# Optimizing a Trainium2 kernel written in Bass

```python
import numpy as np
import jax
import jax.numpy as jnp

def _softmax(x, axis=-1):
    return jax.nn.softmax(x, axis=axis)

def _gelu(x):
    return jax.nn.gelu(x, approximate=True)

def _silu(x):
    return jax.nn.silu(x)

def _sigmoid(x):
    return jax.nn.sigmoid(x)

def _layernorm(x, axis=-1, eps=1e-05):
    m = jnp.mean(x, axis=axis, keepdims=True)
    v = jnp.var(x, axis=axis, keepdims=True)
    return (x - m) / jnp.sqrt(v + eps)

def _scatter_add(tgt, idx, src, axis=0):
    return tgt.at[idx].add(src)

def _segment_sum(src, seg, n):
    return jax.ops.segment_sum(src, seg, n)
kernel_name = 'mk_adaln_ffn_d1_seqx_r4_f74301'

def setup_inputs(seed: int=0):
    np.random.seed(seed)
    _w = jnp.asarray

    def _rec_inputs():
        import jax
        import jax.numpy as jnp
        _rk = jax.random.key(seed)
        x = -1.394e-06 + 0.9999 * jax.random.normal(jax.random.fold_in(_rk, 1), (16, 256, 512), jnp.float32)
        _lenS = 256 - jax.random.randint(jax.random.fold_in(_rk, 7), (16,), 0, max(1, 256 // 4) + 1, jnp.int32)
        _lenS2 = 256 - jax.random.randint(jax.random.fold_in(_rk, 8), (16,), 0, max(1, 256 // 4) + 1, jnp.int32)
        cond_2048 = -0.00499425 + 1.0058 * jax.random.normal(jax.random.fold_in(_rk, 11), (16, 512), jnp.float32)
        return (x, cond_2048)
    x, cond_2048 = _rec_inputs()

    def _L0_cond_setup():
        import jax, jax.numpy as jnp
        import numpy as np
        B, T, D = (16, 128, 512)
        key = jax.random.key(seed)
        k0, k1, k2, k3 = jax.random.split(key, 4)
        scale = 1.0 / np.sqrt(D)
        return {'initial_state': jax.random.normal(k0, (B, D), jnp.float32), 'inputs': jax.random.normal(k1, (B, T, D), jnp.float32), 'W_ih': jax.random.normal(k2, (D, 3 * D), jnp.float32) * scale, 'W_hh': jax.random.normal(k3, (D, 3 * D), jnp.float32) * scale, 'b_ih': jnp.zeros((3 * D,), jnp.float32), 'b_hh': jnp.zeros((3 * D,), jnp.float32)}
    _L0_cond_all = _L0_cond_setup()
    _L0_cond_in = {k: v for k, v in _L0_cond_all.items() if k in ('W_ih', 'W_hh', 'b_ih', 'b_hh')}
    del _L0_cond_all

    def _L0_ffn_setup():
        import jax, jax.numpy as jnp
        import numpy as np
        IN_F, OUT_F = (512, 512)
        N_EXPERTS, RANK, TOP_K = (8, 128, 2)
        key = jax.random.key(seed)
        k_x, k_r, k_a, k_b = jax.random.split(key, 4)
        hidden_states = jax.random.normal(k_x, (4, 1024, IN_F), dtype=jnp.float32)
        router_w = jax.random.normal(k_r, (IN_F, N_EXPERTS), dtype=jnp.float32) * IN_F ** (-0.5)
        Wa = jax.random.normal(k_a, (N_EXPERTS, IN_F, RANK), dtype=jnp.float32) * IN_F ** (-0.5)
        Wb = jax.random.normal(k_b, (N_EXPERTS, RANK, OUT_F), dtype=jnp.float32) * RANK ** (-0.5)
        return {'hidden_states': hidden_states, 'router_w': router_w, 'Wa': Wa, 'Wb': Wb}
    _L0_ffn_all = _L0_ffn_setup()
    _L0_ffn_in = {k: v for k, v in _L0_ffn_all.items() if k in ('router_w', 'Wa', 'Wb')}
    del _L0_ffn_all
    return {'x': x, 'cond_2048': cond_2048, 'L0_cond_W_ih': _L0_cond_in['W_ih'], 'L0_cond_W_hh': _L0_cond_in['W_hh'], 'L0_cond_b_ih': _L0_cond_in['b_ih'], 'L0_cond_b_hh': _L0_cond_in['b_hh'], 'L0_ffn_router_w': _L0_ffn_in['router_w'], 'L0_ffn_Wa': _L0_ffn_in['Wa'], 'L0_ffn_Wb': _L0_ffn_in['Wb']}

def reference(x, cond_2048, L0_cond_W_ih, L0_cond_W_hh, L0_cond_b_ih, L0_cond_b_hh, L0_ffn_router_w, L0_ffn_Wa, L0_ffn_Wb):
    import jax
    import jax.numpy as jnp

    def _L0_cond_ref(initial_state, inputs, W_ih, W_hh, b_ih, b_hh):
        import jax, jax.numpy as jnp
        import numpy as np
        B, T, D = (16, 128, 512)
        "ScanOverTime(GRU cell): sequential per-timestep module call with\n            dict-state passing; merge_dict_trees stacks the per-step\n            'state_predicted' tensors along axis=1 -> [B, T, D]."

        def cell(h, x):
            gi = x @ W_ih + b_ih
            gh = h @ W_hh + b_hh
            i_r, i_z, i_n = jnp.split(gi, 3, axis=-1)
            h_r, h_z, h_n = jnp.split(gh, 3, axis=-1)
            r = jax.nn.sigmoid(i_r + h_r)
            z = jax.nn.sigmoid(i_z + h_z)
            n = jnp.tanh(i_n + r * h_n)
            h_new = (1.0 - z) * n + z * h
            return (h_new, h_new)
        xs = jnp.swapaxes(inputs, 0, 1)
        _, hs = jax.lax.scan(cell, initial_state, xs)
        return jnp.swapaxes(hs, 0, 1)

    def _L0_ffn_ref(hidden_states, router_w, Wa, Wb):
        import jax, jax.numpy as jnp
        import numpy as np
        IN_F, OUT_F = (512, 512)
        N_EXPERTS, RANK, TOP_K = (8, 128, 2)
        B, S, D = hidden_states.shape
        x = hidden_states.reshape(-1, D)
        norm = jnp.maximum(jnp.linalg.norm(x, axis=-1, keepdims=True), 1e-12)
        router_logits = x / norm @ router_w
        routing_weights = jax.nn.softmax(router_logits.astype(jnp.float32), axis=-1)
        rw, selected_experts = jax.lax.top_k(routing_weights, TOP_K)
        rw = rw / jnp.sum(rw, axis=-1, keepdims=True)
        rw = rw.astype(hidden_states.dtype)
        combine = jnp.sum(jax.nn.one_hot(selected_experts, N_EXPERTS, dtype=rw.dtype) * rw[..., None], axis=1)
        out = jnp.zeros((x.shape[0], OUT_F), dtype=hidden_states.dtype)
        for e in range(N_EXPERTS):
            out = out + combine[:, e, None] * (x @ Wa[e] @ Wb[e])
        return out.reshape(B, S, OUT_F)
    x = x + _L0_ffn_ref(_L0_cond_ref(cond_2048, x, L0_cond_W_ih, L0_cond_W_hh, L0_cond_b_ih, L0_cond_b_hh), L0_ffn_router_w, L0_ffn_Wa, L0_ffn_Wb)
    return x

_drawn_inputs = setup_inputs


def setup_inputs(seed=0):
    import zlib

    import numpy as np

    out = dict(_drawn_inputs(seed))
    spreads = {'L0_cond_b_ih': (0.0, 0.1), 'L0_cond_b_hh': (0.0, 0.1)}
    factors = {}
    for name, (base, spread) in spreads.items():
        noise = np.random.default_rng([zlib.crc32(name.encode()), seed]).standard_normal(out[name].shape)
        drawn = base * np.exp(spread * noise) if base else spread * noise
        out[name] = jnp.asarray(drawn.astype(out[name].dtype))
    for name, factor in factors.items():
        out[name] = (out[name] * factor).astype(out[name].dtype)
    return out
```

```python
from contextlib import ExitStack

import concourse.bass as bass
from concourse import mybir

F32 = mybir.dt.float32
F16 = mybir.dt.float16
BF16 = mybir.dt.bfloat16
U32 = mybir.dt.uint32
ALU = mybir.AluOpType
ACT = mybir.ActivationFunctionType

P = 128
PART_SCALE = 128.0
PROD_SCALE = PART_SCALE * PART_SCALE
TERMS = ((0, 0), (0, 1), (1, 0))
NORM_FLOOR = 1e-12


def wait(eng, sem, value):
    if isinstance(value, int) and value <= 0:
        return
    eng.wait_ge(sem, value)


def gru_moe_kernel(nc, x, cond, W_ih, W_hh, b_ih, b_hh, router_w, Wa, Wb, out):
    B, T, D = x.shape
    NE, _, R = Wa.shape
    K = D // P
    S = P // B
    NB = T // S
    G = 3 * P
    assert B * 2 == 32 and R == P and D == K * P and K == 4 and NE == S == 8

    x_blocks = x.rearrange("b (n t) d -> n t b d", t=S)
    out_blocks = out.rearrange("b (n t) d -> n t b d", t=S)

    with ExitStack() as ctx:
        def sb(name, shape, dt=F32):
            return ctx.enter_context(nc.sbuf_tensor(name, shape, dt))

        def ps(name, shape):
            return ctx.enter_context(nc.psum_tensor(name, shape, F32))

        def sem(name):
            return ctx.enter_context(nc.semaphore(name))

        whh32 = sb("whh32", [P, K, 3, K, P])
        wih32 = sb("wih32", [P, K, 3, K, P])
        wa32 = wih32[:, :, :, :, :].rearrange("p k g j c -> p (k g j c)")[:, 0:K * NE * R].rearrange(
            "p (k e r) -> p k e r", k=K, e=NE)
        wb32 = whh32[:, :, :, :, :].rearrange("p k g j c -> p (k g j c)")[:, 0:NE * D].rearrange(
            "p (e n) -> p e n", e=NE)
        rw32 = sb("rw32", [P, K, NE])
        whh = sb("whh", [P, 2, K, K, G], F16)
        wih = sb("wih", [P, 2, K, K, G], F16)
        wa = sb("wa", [P, 2, K, NE, R], F16)
        wb = sb("wb", [P, 2, NE, D], F16)
        rw = sb("rw", [P, 2, K, NE], F16)
        bias32 = sb("bias32", [2, K, 4, P])
        bias_rest = sb("bias_rest", [2, K * 4 * P])
        bias_part = sb("bias_part", [2, K * 4 * P], BF16)
        bias_rows = sb("bias_rows", [P, K, 4 * P], BF16)
        bias_ones = sb("bias_ones", [P, 32], BF16)
        ident = sb("ident", [P, P])
        ones = sb("ones", [P, 1])
        half_pow = sb("half_pow", [P, 1])
        expert_no = sb("expert_no", [P, NE])
        cond_sb = sb("cond_sb", [B, D])
        xin = sb("xin", [P, D])
        xp = sb("xp", [P, 2, K, P], F16)
        st = sb("st", [P, 2, 2, K, 32], F16)
        hist = sb("hist", [P, K, S, B])
        rz = sb("rz", [P, 2 * P])
        omz = sb("omz", [P, P])
        rhn = sb("rhn", [P, P])
        npre = sb("npre", [P, P])
        nn = sb("nn", [P, P])
        u = sb("u", [P, P])
        v = sb("v", [P, K, B])
        hf = sb("hf", [P, 2, K, P], F16)
        sq = sb("sq", [P, K * P])
        sq2 = sb("sq2", [P, 2 * P])
        sqs = sb("sqs", [P, P])
        logit = sb("logit", [P, NE])
        ssum = sb("ssum", [P, 1])
        norm = sb("norm", [P, 1])
        normf = sb("normf", [P, 1])
        rnorm = sb("rnorm", [P, 1])
        top = sb("top", [P, 8])
        top_at = sb("top_at", [P, 8], U32)
        top_no = sb("top_no", [P, 8])
        gap = sb("gap", [P, 2])
        wt = sb("wt", [P, 2])
        wts = sb("wts", [P, 2])
        pick = sb("pick", [P, 2, NE])
        comb = sb("comb", [P, NE])
        y = sb("y", [P, 2, 2, P], F16)
        xres = sb("xres", [P, D])
        acc = sb("acc", [P, D])
        outb = sb("outb", [P, D])
        gates = [ps(f"gates{i}", [P, 4 * P]) for i in range(2)]
        turned = ps("turned", [P, 4 * P])
        xturn = ps("xturn", [P, 4 * P])
        ybank = [ps(f"ybank{i}", [P, 4 * P]) for i in range(2)]
        obank = ps("obank", [P, 4 * P])
        rbank = ps("rbank", [P, 4 * P])

        zT = turned[:, 0:P].rearrange("p (k c) -> p k c", c=32)
        uT = turned[:, P:2 * P].rearrange("p (k c) -> p k c", c=32)
        c0T = turned[:, 0:K * B].rearrange("p (k c) -> p k c", c=B)

        consts_ready = sem("consts_ready")
        small_loaded = sem("small_loaded")
        whh_loaded, wih_loaded, wa_loaded, wb_loaded = (sem(f"w{n}_loaded") for n in ("hh", "ih", "a", "b"))
        hi_split = sem("hi_split")
        weights_split = sem("weights_split")
        bias_step = sem("bias_step")
        xin_loaded = sem("xin_loaded")
        c0_turned = sem("c0_turned")
        x_turned = sem("x_turned")
        xhi_ready = sem("xhi_ready")
        xlo_ready = sem("xlo_ready")
        xpart_done = sem("xpart_done")
        gates_done = sem("gates_done")
        rz_ready = sem("rz_ready")
        omz_ready = sem("omz_ready")
        rhn_ready = sem("rhn_ready")
        npre_ready = sem("npre_ready")
        n_ready = sem("n_ready")
        z_turned = sem("z_turned")
        v_ready = sem("v_ready")
        u_ready = sem("u_ready")
        u_turned = sem("u_turned")
        hhi_ready = sem("hhi_ready")
        h_ready = sem("h_ready")
        hlo_ready = sem("hlo_ready")
        hfhi_ready = sem("hfhi_ready")
        hflo_ready = sem("hflo_ready")
        sq_step = sem("sq_step")
        logits_done = sem("logits_done")
        ssum_done = sem("ssum_done")
        router_read = sem("router_read")
        top_step = sem("top_step")
        norm_ready = sem("norm_ready")
        rnorm_step = sem("rnorm_step")
        wt_ready = sem("wt_ready")
        comb_step = sem("comb_step")
        y_done = sem("y_done")
        yhi_ready = sem("yhi_ready")
        ylo_ready = sem("ylo_ready")
        o_done = sem("o_done")
        acc_done = sem("acc_done")
        xres_loaded = sem("xres_loaded")
        out_sent = sem("out_sent")

        N_CONST = 7
        SQ_STEPS, TOP_STEPS, RN_STEPS, COMB_STEPS = 3, 5, 2, 4
        SPLITS = []
        for k in range(K):
            for g in range(3):
                SPLITS.append((whh_loaded, whh32[:, k, g, :, :],
                               [whh[:, p, k, :, g * P:(g + 1) * P] for p in range(2)]))
        N_HH_SPLITS = len(SPLITS)
        for k in range(K):
            for g in range(3):
                r0 = (g + 1) % 3 * P
                SPLITS.append((wih_loaded, wih32[:, k, g, :, :],
                               [wih[:, p, k, :, r0:r0 + P] for p in range(2)]))
        N_GRU_SPLITS = len(SPLITS)
        SPLITS.append((small_loaded, rw32[:, :, :], [rw[:, p, :, :] for p in range(2)]))
        for e in range(0, NE, 2):
            SPLITS.append((wb_loaded, wb32[:, e:e + 2, :], [wb[:, p, e:e + 2, :] for p in range(2)]))
        for k in range(K):
            SPLITS.append((wa_loaded, wa32[:, k, :, :], [wa[:, p, k, :, :] for p in range(2)]))
        LOADED = {whh_loaded: 16, wih_loaded: 16, small_loaded: 16 * 8, wb_loaded: 16, wa_loaded: 16 * K}
        N_SMALL = 16 * 8

        block = ctx.enter_context(nc.Block())

        @block.sync
        def _(sp):
            def load_x(blk, n):
                wait(sp, x_turned, n)
                sp.dma_start(xin[:, :], x_blocks[blk]).then_inc(xin_loaded, 16)

            def load_residual(f):
                wait(sp, acc_done, f * NE)
                sp.dma_start(xres[:, :], x_blocks[f]).then_inc(xres_loaded, 16)

            def store(f):
                wait(sp, acc_done, (f + 1) * NE)
                sp.dma_start(out_blocks[f], outb[:, :]).then_inc(out_sent, 16)

            load_x(0, 0)
            sp.dma_start(cond_sb[:, :], cond).then_inc(small_loaded, 16)
            sp.dma_start(whh32[:, :, :, :, :].rearrange("p k g j c -> p k (g j c)"),
                         W_hh.rearrange("(k p) n -> p k n", p=P)).then_inc(whh_loaded, 16)
            wait(sp, consts_ready, N_CONST)
            for row, b, gs in ((0, b_ih, ((0, 1), (1, 2), (2, 0))), (1, b_hh, ((0, 1), (1, 2), (2, 3)))):
                for g, region in gs:
                    sp.dma_start(bias32[row:row + 1, :, region, :],
                                 b[g * D:(g + 1) * D].rearrange("(a j c) -> a j c", a=1, c=P)
                                 ).then_inc(small_loaded, 16)
            sp.dma_start(rw32[:, :, :], router_w.rearrange("(k p) e -> p k e", p=P)).then_inc(small_loaded, 16)
            load_x(1, 1)
            wait(sp, weights_split, N_HH_SPLITS)
            sp.dma_start(wb32, Wb.rearrange("e r n -> r e n")).then_inc(wb_loaded, 16)
            wait(sp, weights_split, N_GRU_SPLITS)
            for k in range(K):
                sp.dma_start(wa32[:, k, :, :], Wa[:, k * P:(k + 1) * P, :].rearrange("e p r -> p e r")
                             ).then_inc(wa_loaded, 16)
            with sp.Fori(1, NB - 1) as i:
                load_x(i + 1, i + 1)
                load_residual(i - 1)
                store(i - 1)
            load_x(0, NB)
            load_residual(NB - 2)
            store(NB - 2)
            load_residual(NB - 1)
            store(NB - 1)
            wait(sp, out_sent, 16 * NB)

        @block.gpsimd
        def _(pool):
            nc.gpsimd.memset(bias32[:, :, :, :], 0.0).then_inc(consts_ready, 1)
            nc.gpsimd.memset(bias_rows[:, :, :], 0.0).then_inc(consts_ready, 1)
            nc.gpsimd.memset(bias_ones[:, :], PROD_SCALE).then_inc(consts_ready, 1)
            nc.gpsimd.memset(st[:, :, :, :, :], 0.0).then_inc(consts_ready, 1)
            nc.gpsimd.memset(ones[:, :], 1.0).then_inc(consts_ready, 1)
            nc.gpsimd.memset(half_pow[:, :], 0.5).then_inc(consts_ready, 1)
            nc.gpsimd.memset(ident[:, :], 0.0).then_inc(consts_ready, 1)
            pool.wait_ge(consts_ready, N_CONST)
            nc.gpsimd.affine_select(out=ident[:, :], in_=ident[:, :], compare_op=ALU.not_equal, fill=1.0,
                                    base=0, pattern=[[-1, P]], channel_multiplier=1).then_inc(consts_ready, 1)
            nc.gpsimd.iota(expert_no[:, :], pattern=[[1, NE]], base=0, channel_multiplier=0,
                           allow_small_or_imprecise_dtypes=True).then_inc(consts_ready, 1)

            def square(f):
                wait(pool, h_ready, (f + 1) * S + 1)
                h = hist[:, :, :, :].rearrange("p k s b -> p (k s b)")
                nc.gpsimd.tensor_tensor(sq[:, :], h, h, ALU.mult).then_inc(sq_step, 1)
                wait(pool, sq_step, f * SQ_STEPS + 1)
                nc.gpsimd.tensor_tensor(sq2[:, :], sq[:, 0:2 * P], sq[:, 2 * P:4 * P], ALU.add).then_inc(sq_step, 1)
                wait(pool, sq_step, f * SQ_STEPS + 2)
                wait(pool, ssum_done, f)
                nc.gpsimd.tensor_tensor(sqs[:, :], sq2[:, 0:P], sq2[:, P:2 * P], ALU.add).then_inc(sq_step, 1)

            def root(f):
                wait(pool, router_read, 2 * (f + 1))
                nc.gpsimd.tensor_tensor(norm[:, :], ssum[:, :], half_pow[:, :], ALU.pow).then_inc(norm_ready, 1)

            with pool.Fori(1, NB + 1) as i:
                square(i - 1)
                root(i - 1)

        @block.scalar
        def _(act):
            act.dma_start(wih32[:, :, :, :, :].rearrange("p k g j c -> p k (g j c)"),
                          W_ih.rearrange("(k p) n -> p k n", p=P)).then_inc(wih_loaded, 16)

            def split_x(n):
                wait(act, x_turned, n + 1)
                wait(act, xpart_done, n * S // 2)
                nc.scalar.activation(xp[:, 0, :, :].rearrange("p k c -> p (k c)"), xturn[:, :], ACT.Copy,
                                     scale=PART_SCALE).then_inc(xhi_ready, 1)

            def gru_step(n, s):
                g = gates[s // 2 % 2]
                wait(act, gates_done, n + 1)
                nc.scalar.activation(rz[:, :], g[:, P:3 * P], ACT.Sigmoid, scale=1 / PROD_SCALE).then_inc(rz_ready, 1)
                wait(act, rz_ready, n + 1)
                nc.scalar.activation(omz[:, :], rz[:, P:2 * P], ACT.Copy, scale=-PART_SCALE,
                                     bias=PART_SCALE).then_inc(omz_ready, 1)
                wait(act, npre_ready, n + 1)
                nc.scalar.activation(nn[:, :], npre[:, :], ACT.Tanh, scale=1 / PROD_SCALE).then_inc(n_ready, 1)

            def split_states(f):
                wait(act, h_ready, (f + 1) * S + 1)
                wait(act, y_done, f * NE)
                nc.scalar.activation(hf[:, 0, :, :], hist[:, :, :, :].rearrange("p k s b -> p k (s b)"),
                                     ACT.Copy).then_inc(hfhi_ready, 1)

            def split_y(m, e):
                wait(act, y_done, m + 1)
                wait(act, o_done, m - 1 if e else m)
                nc.scalar.activation(y[:, e % 2, 0, :], ybank[e % 2][:, 0:P], ACT.Copy,
                                     scale=1 / PART_SCALE).then_inc(yhi_ready, 1)

            def weigh(f):
                wait(act, rnorm_step, (f + 1) * RN_STEPS)
                wait(act, top_step, (f + 1) * TOP_STEPS)
                nc.scalar.activation(wt[:, :], gap[:, :], ACT.Sigmoid, scale=rnorm[:, :]).then_inc(wt_ready, 1)

            def block_of(i, gru=True, ffn=True):
                for s in range(S):
                    if s == 0 and ffn:
                        split_states(i - 1)
                    if gru:
                        gru_step(i * S + s, s)
                        if s == 5:
                            split_x(i + 1)
                    if not ffn:
                        split_weights(N_GRU_SPLITS + s)
                        if s == 7:
                            split_weights(N_GRU_SPLITS + 8)
                    if ffn:
                        if s <= 6:
                            split_y((i - 1) * NE + s, s)
                        if s == 1:
                            weigh(i - 1)
                        if s == 6:
                            split_y((i - 1) * NE + 7, 7)

            def split_weights(n):
                loaded, src, (hi, _) = SPLITS[n]
                wait(act, loaded, LOADED[loaded])
                nc.scalar.activation(hi, src, ACT.Copy, scale=PART_SCALE).then_inc(hi_split, 1)

            split_x(0)
            for n in range(N_GRU_SPLITS):
                split_weights(n)
            block_of(0, ffn=False)
            with act.Fori(1, NB) as i:
                block_of(i)
            block_of(NB, gru=False)

        @block.vector
        def _(dve):
            def split_x(n):
                wait(dve, xhi_ready, n + 1)
                nc.vector.scalar_tensor_tensor(out=xp[:, 1, :, :].rearrange("p k c -> p (k c)"), in0=xturn[:, :],
                                               scalar=PART_SCALE, in1=xp[:, 0, :, :].rearrange("p k c -> p (k c)"),
                                               op0=ALU.mult, op1=ALU.subtract).then_inc(xlo_ready, 1)

            def gru_step(n, s, i, ffn):
                g = gates[s // 2 % 2]
                q, q1 = s % 2, (s + 1) % 2
                wait(dve, rz_ready, n + 1)
                nc.vector.tensor_tensor(rhn[:, :], rz[:, 0:P], g[:, 3 * P:4 * P], ALU.mult).then_inc(rhn_ready, 1)
                wait(dve, rhn_ready, n + 1)
                nc.vector.tensor_tensor(npre[:, :], rhn[:, :], g[:, 0:P], ALU.add).then_inc(npre_ready, 1)
                wait(dve, z_turned, n + 1)
                nc.vector.tensor_tensor(v[:, :, :], zT[:, :, B * q:B * q + B], hist[:, :, (s - 1) % S, :],
                                        ALU.mult).then_inc(v_ready, 1)
                wait(dve, omz_ready, n + 1)
                wait(dve, n_ready, n + 1)
                nc.vector.tensor_tensor(u[:, :], omz[:, :], nn[:, :], ALU.mult).then_inc(u_ready, 1)
                wait(dve, v_ready, n + 1)
                wait(dve, u_turned, n + 1)
                uTq = uT[:, :, B * q:B * q + B]
                nc.vector.tensor_tensor(st[:, q1, 0, :, B * q1:B * q1 + B], uTq, v[:, :, :],
                                        ALU.add).then_inc(hhi_ready, 1)
                if s == 0 and ffn:
                    wait(dve, hfhi_ready, i)
                    wait(dve, hflo_ready, i)
                    wait(dve, sq_step, (i - 1) * SQ_STEPS + 1)
                nc.vector.tensor_tensor(hist[:, :, s, :], uTq, v[:, :, :], ALU.add).then_inc(h_ready, 1)
                wait(dve, h_ready, n + 2)
                wait(dve, hhi_ready, n + 2)
                nc.vector.tensor_tensor(st[:, q1, 1, :, B * q1:B * q1 + B], hist[:, :, s, :],
                                        st[:, q1, 0, :, B * q1:B * q1 + B], ALU.subtract).then_inc(hlo_ready, 1)

            def split_states(f):
                wait(dve, hfhi_ready, f + 1)
                nc.vector.tensor_tensor(hf[:, 1, :, :], hist[:, :, :, :].rearrange("p k s b -> p k (s b)"),
                                        hf[:, 0, :, :], ALU.subtract).then_inc(hflo_ready, 1)

            def split_y(m, e):
                wait(dve, yhi_ready, m + 1)
                nc.vector.scalar_tensor_tensor(out=y[:, e % 2, 1, :], in0=ybank[e % 2][:, 0:P],
                                               scalar=1 / PART_SCALE, in1=y[:, e % 2, 0, :],
                                               op0=ALU.mult, op1=ALU.subtract).then_inc(ylo_ready, 1)

            def rank_experts(f):
                wait(dve, logits_done, f + 1)
                wait(dve, ssum_done, f + 1)
                nc.vector.tensor_copy(logit[:, :], rbank[:, 0:NE]).then_inc(router_read, 1)
                wait(dve, router_read, 2 * f + 1)
                nc.vector.tensor_copy(ssum[:, :], rbank[:, NE:NE + 1]).then_inc(router_read, 1)
                nc.vector.max(top[:, :], logit[:, :]).then_inc(top_step, 1)
                t0 = f * TOP_STEPS
                wait(dve, top_step, t0 + 1)
                nc.vector.tensor_tensor(gap[:, 0:1], top[:, 0:1], top[:, 1:2], ALU.subtract).then_inc(top_step, 1)
                nc.vector.tensor_tensor(gap[:, 1:2], top[:, 1:2], top[:, 0:1], ALU.subtract).then_inc(top_step, 1)
                nc.vector.max_index(top_at[:, :], top[:, :], logit[:, :]).then_inc(top_step, 1)
                wait(dve, top_step, t0 + 4)
                nc.vector.tensor_copy(top_no[:, :], top_at[:, :]).then_inc(top_step, 1)

            def invert_norm(f):
                r0 = f * RN_STEPS
                wait(dve, norm_ready, f + 1)
                nc.vector.tensor_scalar(normf[:, :], norm[:, :], NORM_FLOOR * PART_SCALE, PART_SCALE,
                                        ALU.max, ALU.mult).then_inc(rnorm_step, 1)
                wait(dve, rnorm_step, r0 + 1)
                nc.vector.reciprocal(rnorm[:, :], normf[:, :]).then_inc(rnorm_step, 1)

            def combine(f):
                c0 = f * COMB_STEPS
                wait(dve, wt_ready, f + 1)
                nc.vector.tensor_scalar(wts[:, :], wt[:, :], 1 / PROD_SCALE, None, ALU.mult).then_inc(comb_step, 1)
                wait(dve, top_step, (f + 1) * TOP_STEPS)
                wait(dve, comb_step, c0 + 1)
                for t in range(2):
                    nc.vector.tensor_scalar(pick[:, t, :], expert_no[:, :], top_no[:, t:t + 1], wts[:, t:t + 1],
                                            ALU.is_equal, ALU.mult).then_inc(comb_step, 1)
                wait(dve, comb_step, c0 + 3)
                nc.vector.tensor_tensor(comb[:, :], pick[:, 0, :], pick[:, 1, :], ALU.add).then_inc(comb_step, 1)

            def add_expert(f, e):
                m = f * NE + e
                bank = rbank if e == NE - 1 else obank
                wait(dve, o_done, m + 1)
                if e == 0:
                    wait(dve, comb_step, (f + 1) * COMB_STEPS)
                    wait(dve, xres_loaded, 16 * (f + 1))
                if e == NE - 1:
                    wait(dve, out_sent, 16 * f)
                wait(dve, acc_done, m)
                nc.vector.scalar_tensor_tensor(out=(outb if e == NE - 1 else acc)[:, :], in0=bank[:, :],
                                               scalar=comb[:, e:e + 1], in1=(xres if e == 0 else acc)[:, :],
                                               op0=ALU.mult, op1=ALU.add).then_inc(acc_done, 1)

            def block_of(i, gru=True, ffn=True):
                f = i - 1
                for s in range(S):
                    if s == 0 and ffn:
                        split_states(f)
                    if gru:
                        gru_step(i * S + s, s, i, ffn)
                        if s == 5:
                            split_x(i + 1)
                    if not ffn:
                        split_weights(N_GRU_SPLITS + s)
                        if s == 7:
                            split_weights(N_GRU_SPLITS + 8)
                    if ffn:
                        if s <= 6:
                            split_y(f * NE + s, s)
                        if s == 6:
                            split_y(f * NE + 7, 7)
                        if s == 0:
                            rank_experts(f)
                        if s == 1:
                            invert_norm(f)
                            combine(f)
                        if s >= 1:
                            add_expert(f, s - 1)
                        if s == 7:
                            add_expert(f, 7)

            dve.wait_ge(small_loaded, N_SMALL)
            dve.wait_ge(consts_ready, N_CONST + 2)
            rows = bias_rows[:, :, :].rearrange("p k c -> p (k c)")
            src = bias32[:, :, :, :].rearrange("p j g c -> p (j g c)")
            for n in range(3):
                nc.vector.tensor_copy(bias_part[:, :], src).then_inc(bias_step, 1)
                dve.wait_ge(bias_step, 3 * n + 1)
                nc.vector.tensor_copy(rows[32 * n:32 * n + 2, :], bias_part[:, :]).then_inc(bias_step, 1)
                nc.vector.tensor_tensor(bias_rest[:, :], src, bias_part[:, :], ALU.subtract).then_inc(bias_step, 1)
                dve.wait_ge(bias_step, 3 * n + 3)
                src = bias_rest[:, :]
            dve.wait_ge(c0_turned, 1)
            nc.vector.tensor_scalar(hist[:, :, S - 1, :], c0T, PART_SCALE, None, ALU.mult).then_inc(h_ready, 1)
            dve.wait_ge(h_ready, 1)
            nc.vector.tensor_copy(st[:, 0, 0, :, 0:B], hist[:, :, S - 1, :]).then_inc(hhi_ready, 1)
            dve.wait_ge(hhi_ready, 1)
            nc.vector.tensor_tensor(st[:, 0, 1, :, 0:B], hist[:, :, S - 1, :], st[:, 0, 0, :, 0:B],
                                    ALU.subtract).then_inc(hlo_ready, 1)
            def split_weights(n):
                _, src, (hi, lo) = SPLITS[n]
                wait(dve, hi_split, n + 1)
                nc.vector.scalar_tensor_tensor(out=lo, in0=src, scalar=PART_SCALE, in1=hi, op0=ALU.mult,
                                               op1=ALU.subtract).then_inc(weights_split, 1)

            split_x(0)
            for n in range(N_GRU_SPLITS):
                split_weights(n)
            block_of(0, ffn=False)
            with dve.Fori(1, NB) as i:
                block_of(i)
            block_of(NB, gru=False)

        @block.tensor
        def _(pe):
            def turn_x(n):
                wait(pe, xin_loaded, 16 * (n + 1))
                wait(pe, xlo_ready, n)
                for k in range(K):
                    mm = nc.tensor.transpose(xturn[:, k * P:(k + 1) * P], xin[:, k * P:(k + 1) * P], ident[:, :])
                mm.then_inc(x_turned, 1)

            def x_half(pair, half, blk):
                g = gates[pair % 2]
                if half == 0:
                    if pair % (S // 2) == 0:
                        wait(pe, xhi_ready, blk + 1)
                        wait(pe, xlo_ready, blk + 1)
                    for j in range(K):
                        nc.tensor.matmul(g[32 * j:32 * j + 32, :], bias_ones[:, :], bias_rows[:, j, :],
                                         start=True, stop=False, skip_group_check=True)
                c = 32 * (pair % (S // 2))
                for k in range(2 * half, 2 * half + 2):
                    for ph, pw in TERMS:
                        for j in range(K):
                            mm = nc.tensor.matmul(g[32 * j:32 * j + 32, 0:G], xp[:, ph, k, c:c + 32],
                                                  wih[:, pw, k, j, :], start=False, stop=False,
                                                  skip_group_check=True)
                if half == 1:
                    mm.then_inc(xpart_done, 1)

            def state_part(n, s):
                g = gates[s // 2 % 2]
                for ph, pw in TERMS:
                    if pw == 0:
                        wait(pe, (hhi_ready, hlo_ready)[ph], n + 1)
                    for k in range(K):
                        for j in range(K):
                            mm = nc.tensor.matmul(g[32 * j:32 * j + 32, P:4 * P], st[:, s % 2, ph, k, :],
                                                  whh[:, pw, k, j, :], start=False, stop=True,
                                                  skip_group_check=True)
                mm.then_inc(gates_done, 1)

            def logits(f):
                wait(pe, hfhi_ready, f + 1)
                wait(pe, hflo_ready, f + 1)
                wait(pe, acc_done, f * NE)
                n = 0
                for k in range(K):
                    for ph, pw in TERMS:
                        mm = nc.tensor.matmul(rbank[:, 0:NE], hf[:, ph, k, :], rw[:, pw, k, :], start=(n == 0),
                                              stop=(n == 3 * K - 1), skip_group_check=True)
                        n += 1
                mm.then_inc(logits_done, 1)

            def sum_squares(f):
                wait(pe, sq_step, (f + 1) * SQ_STEPS)
                nc.tensor.matmul(rbank[:, NE:NE + 1], sqs[:, :], ones[:, :], start=False, stop=True,
                                 skip_group_check=True).then_inc(ssum_done, 1)

            def expert_down(f, e):
                m = f * NE + e
                wait(pe, ylo_ready, m - 1 if e else m)
                n = 0
                for k in range(K):
                    for ph, pw in TERMS:
                        mm = nc.tensor.matmul(ybank[e % 2][:, 0:P], wa[:, pw, k, e, :], hf[:, ph, k, :],
                                              start=(n == 0), stop=(n == 3 * K - 1))
                        n += 1
                mm.then_inc(y_done, 1)

            def expert_up(f, e):
                m = f * NE + e
                bank = rbank if e == NE - 1 else obank
                wait(pe, ylo_ready, m + 1)
                wait(pe, acc_done, m - 1 if e == NE - 1 else m)
                for n, (ph, pw) in enumerate(TERMS):
                    mm = nc.tensor.matmul(bank[:, :], y[:, e % 2, ph, :], wb[:, pw, e, :], start=(n == 0),
                                          stop=(n == 2))
                mm.then_inc(o_done, 1)

            def block_of(i, gru=True, ffn=True):
                f = i - 1
                for s in range(S):
                    n = i * S + s
                    if gru:
                        state_part(n, s)
                    if ffn:
                        if s == 0:
                            logits(f)
                        if s <= 6:
                            expert_down(f, s)
                        if s == 6:
                            expert_down(f, 7)
                        if s == 7:
                            expert_up(f, 6)
                    if gru:
                        wait(pe, rz_ready, n + 1)
                        nc.tensor.transpose(turned[:, 0:P], rz[:, P:2 * P], ident[:, :]).then_inc(z_turned, 1)
                        if s == 4:
                            turn_x(i + 1)
                        x_half(s // 2 + 1, s % 2, i + 1)
                        wait(pe, v_ready, n + 1)
                        wait(pe, u_ready, n + 1)
                        nc.tensor.transpose(turned[:, P:2 * P], u[:, :], ident[:, :]).then_inc(u_turned, 1)
                    if ffn:
                        if s == 0:
                            sum_squares(f)
                        if 1 <= s <= 6:
                            expert_up(f, s - 1)
                        if s == 7:
                            expert_up(f, 7)

            pe.wait_ge(consts_ready, N_CONST + 2)
            pe.wait_ge(xin_loaded, 16)
            pe.wait_ge(small_loaded, N_SMALL)
            for k in range(K):
                mm = nc.tensor.transpose(turned[:, k * B:(k + 1) * B], cond_sb[:, k * P:(k + 1) * P], ident[0:B, 0:B])
            mm.then_inc(c0_turned, 1)
            turn_x(0)
            pe.wait_ge(bias_step, 9)
            pe.wait_ge(weights_split, N_GRU_SPLITS)
            x_half(0, 0, 0)
            x_half(0, 1, 0)
            block_of(0, ffn=False)
            pe.wait_ge(weights_split, len(SPLITS))
            with pe.Fori(1, NB) as i:
                block_of(i)
            block_of(NB, gru=False)


_INS = ['x', 'cond_2048', 'L0_cond_W_ih', 'L0_cond_W_hh', 'L0_cond_b_ih', 'L0_cond_b_hh', 'L0_ffn_router_w',
        'L0_ffn_Wa', 'L0_ffn_Wb']


def kernel(**inputs):
    import numpy as np
    import concourse.bacc as bacc
    from concourse.bass_utils import run_bass_kernel_spmd

    nc = bacc.Bacc("TRN2", target_bir_lowering=False, num_devices=1)
    arrays, args = {}, []
    for name in _INS:
        a = np.ascontiguousarray(inputs[name])
        arrays[f"in_{name}"] = a
        args.append(nc.dram_tensor(f"in_{name}", a.shape, mybir.dt.from_np(a.dtype), kind="ExternalInput").ap())
    shape = inputs['x'].shape
    args.append(nc.dram_tensor("out_0", shape, F32, kind="ExternalOutput").ap())
    gru_moe_kernel(nc, *args)
    return run_bass_kernel_spmd(nc, [arrays], core_ids=[0]).results[0]["out_0"]
```

```python
from contextlib import ExitStack

import concourse.bass as bass
from concourse import mybir

F32 = mybir.dt.float32
F16 = mybir.dt.float16
BF16 = mybir.dt.bfloat16
U32 = mybir.dt.uint32
ALU = mybir.AluOpType
ACT = mybir.ActivationFunctionType

P = 128
PART_SCALE = 128.0
PROD_SCALE = PART_SCALE * PART_SCALE
TERMS = ((0, 0), (0, 1), (1, 0))
NORM_FLOOR = 1e-12


def wait(eng, sem, value):
    if isinstance(value, int) and value <= 0:
        return
    eng.wait_ge(sem, value)


def gru_moe_kernel(nc, x, cond, W_ih, W_hh, b_ih, b_hh, router_w, Wa, Wb, out):
    B, T, D = x.shape
    NE, _, R = Wa.shape
    K = D // P
    S = P // B
    NB = T // S
    G = 3 * P
    assert B * 2 == 32 and R == P and D == K * P and K == 4 and NE == S == 8

    x_blocks = x.rearrange("b (n t) d -> n t b d", t=S)
    x_parts = x.rearrange("b (n r q) (j c) -> n j q b r c", q=2, r=S // 2, j=K)
    out_blocks = out.rearrange("b (n t) d -> n t b d", t=S)

    with ExitStack() as ctx:
        def sb(name, shape, dt=F32):
            return ctx.enter_context(nc.sbuf_tensor(name, shape, dt))

        def ps(name, shape):
            return ctx.enter_context(nc.psum_tensor(name, shape, F32))

        def sem(name):
            return ctx.enter_context(nc.semaphore(name))

        whh32 = sb("whh32", [P, K, 3, K, P])
        wih32 = sb("wih32", [P, K, 3, K, P])
        wa32 = wih32[:, :, :, :, :].rearrange("p k g j c -> p (k g j c)")[:, 0:K * NE * R].rearrange(
            "p (k e r) -> p k e r", k=K, e=NE)
        wb32 = whh32[:, :, :, :, :].rearrange("p k g j c -> p (k g j c)")[:, 0:NE * D].rearrange(
            "p (e n) -> p e n", e=NE)
        rw32 = sb("rw32", [P, K, NE])
        whh = sb("whh", [P, 2, K, K, G], F16)
        wih = sb("wih", [P, 2, K, K, G], F16)
        wa = sb("wa", [P, 2, K, NE, R], F16)
        wb = sb("wb", [P, 2, NE, D], F16)
        rw = sb("rw", [P, 2, K, NE], F16)
        bias32 = sb("bias32", [2 * K * 4, P])
        bias_rest = sb("bias_rest", [2 * K * 4, 2, P])
        bias_part = sb("bias_part", [2 * K * 4, 3, P], BF16)
        bias_rows = sb("bias_rows", [P, 4 * P], BF16)
        bias_sel = sb("bias_sel", [P, K, 32], BF16)
        ones = sb("ones", [P, 1])
        half_pow = sb("half_pow", [P, 1])
        expert_no = sb("expert_no", [P, NE])
        cond_sb = sb("cond_sb", [P, P])
        cond_t = sb("cond_t", [P, K, 32])
        xin = sb("xin", [P, S // 2, P])
        xt = sb("xt", [P, S // 2, K, 32])
        xp = sb("xp", [P, 2, S // 2, K, 32], F16)
        st = sb("st", [P, 2, 2, K, 32], F16)
        hist = sb("hist", [P, K, S, B])
        rz = sb("rz", [P, 2 * P])
        omz = sb("omz", [P, P])
        rhn = sb("rhn", [P, P])
        npre = sb("npre", [P, P])
        nn = sb("nn", [P, P])
        u = sb("u", [P, P])
        zt = sb("zt", [P, K, 32])
        ut = sb("ut", [P, K, 32])
        v = sb("v", [P, K, B])
        hf = sb("hf", [P, 2, K, P], F16)
        sq = sb("sq", [P, K * P])
        sq2 = sb("sq2", [P, 2 * P])
        sqs = sb("sqs", [P, P])
        logit = sb("logit", [P, NE])
        ssum = sb("ssum", [P, 1])
        norm = sb("norm", [P, 1])
        normf = sb("normf", [P, 1])
        rnorm = sb("rnorm", [P, 1])
        top = sb("top", [P, 8])
        top_at = sb("top_at", [P, 8], U32)
        top_no = sb("top_no", [P, 8])
        gap = sb("gap", [P, 2])
        wt = sb("wt", [P, 2])
        wts = sb("wts", [P, 2])
        pick = sb("pick", [P, 2, NE])
        comb = sb("comb", [P, NE])
        y = sb("y", [P, 2, 2, P], F16)
        xres = sb("xres", [P, D])
        acc = sb("acc", [P, D])
        outb = sb("outb", [P, D])
        gates = [ps(f"gates{i}", [P, 4 * P]) for i in range(2)]
        ybank = [ps(f"ybank{i}", [P, 4 * P]) for i in range(2)]
        obank = [ps(f"obank{i}", [P, 4 * P]) for i in range(2)]
        rbank = ps("rbank", [P, 4 * P])

        consts_ready = sem("consts_ready")
        cond_loaded = sem("cond_loaded")
        bias_loaded = sem("bias_loaded")
        bias_placed = sem("bias_placed")
        whh_loaded = [sem(f"whh{k}_loaded") for k in range(K)]
        wih_loaded = [sem(f"wih{k}_loaded") for k in range(K)]
        wa_loaded, wb_loaded, rw_loaded = sem("wa_loaded"), sem("wb_loaded"), sem("rw_loaded")
        hi_split = sem("hi_split")
        weights_split = sem("weights_split")
        bias_step = sem("bias_step")
        xin_loaded = sem("xin_loaded")
        cond_turned = sem("cond_turned")
        x_turned = sem("x_turned")
        xhi_ready = sem("xhi_ready")
        xlo_ready = sem("xlo_ready")
        xpart_done = sem("xpart_done")
        gates_done = sem("gates_done")
        rz_ready = sem("rz_ready")
        omz_ready = sem("omz_ready")
        rhn_ready = sem("rhn_ready")
        npre_ready = sem("npre_ready")
        n_ready = sem("n_ready")
        z_turned = sem("z_turned")
        v_ready = sem("v_ready")
        u_ready = sem("u_ready")
        u_turned = sem("u_turned")
        hhi_ready = sem("hhi_ready")
        h_ready = sem("h_ready")
        hlo_ready = sem("hlo_ready")
        hfhi_ready = sem("hfhi_ready")
        hflo_ready = sem("hflo_ready")
        sq_step = sem("sq_step")
        logits_done = sem("logits_done")
        ssum_done = sem("ssum_done")
        router_read = sem("router_read")
        top_step = sem("top_step")
        norm_ready = sem("norm_ready")
        rnorm_step = sem("rnorm_step")
        wt_ready = sem("wt_ready")
        comb_step = sem("comb_step")
        y_done = sem("y_done")
        yhi_ready = sem("yhi_ready")
        ylo_ready = sem("ylo_ready")
        o_done = sem("o_done")
        acc_done = sem("acc_done")
        xres_loaded = sem("xres_loaded")
        out_sent = sem("out_sent")

        N_CONST = 8
        SQ_STEPS, TOP_STEPS, RN_STEPS, COMB_STEPS = 3, 5, 2, 4
        N_XIN = 16 * 2 * K
        SPLITS = []

        def split_ih(k):
            for g in range(3):
                r0 = (g + 1) % 3 * P
                SPLITS.append((wih_loaded[k], 16, wih32[:, k, g, :, :],
                               [wih[:, p, k, :, r0:r0 + P] for p in range(2)]))

        def split_hh(k):
            for g in range(3):
                SPLITS.append((whh_loaded[k], 16, whh32[:, k, g, :, :],
                               [whh[:, p, k, :, g * P:(g + 1) * P] for p in range(2)]))

        split_ih(0)
        for k in range(K):
            split_hh(k)
        for k in range(1, K):
            split_ih(k)
        N_GRU_SPLITS = len(SPLITS)
        BIAS_AT, STATE_AT, X_AFTER = 6, N_GRU_SPLITS - 8, N_GRU_SPLITS - 4
        SPLITS.append((rw_loaded, 16 * K, rw32[:, :, :], [rw[:, p, :, :] for p in range(2)]))
        for e in range(0, NE, 2):
            SPLITS.append((wb_loaded, 16, wb32[:, e:e + 2, :], [wb[:, p, e:e + 2, :] for p in range(2)]))
        for k in range(K):
            SPLITS.append((wa_loaded, 16 * K * K, wa32[:, k, :, :], [wa[:, p, k, :, :] for p in range(2)]))

        LATE_SPLITS = [[N_GRU_SPLITS + n for n in ns] for ns in ([], [0], [1], [2], [3, 4], [5, 6], [7, 8], [])]

        block = ctx.enter_context(nc.Block())

        @block.sync
        def _(sp):
            def load_x(blk, n):
                wait(sp, x_turned, n)
                for j in range(K):
                    for q in range(2):
                        p0 = 32 * j + B * q
                        sp.dma_start(xin[p0:p0 + B, :, :], x_parts[blk, j, q]).then_inc(xin_loaded, 16)

            def load_residual(f):
                wait(sp, acc_done, f * NE)
                sp.dma_start(xres[:, :], x_blocks[f]).then_inc(xres_loaded, 16)

            def store(f):
                wait(sp, acc_done, (f + 1) * NE)
                sp.dma_start(out_blocks[f], outb[:, :]).then_inc(out_sent, 16)

            ih_rows = W_ih.rearrange("(j k c) n -> k j c n", j=K, k=K)

            def load_ih(k):
                sp.dma_start(wih32[:, k, :, :, :].rearrange("p g j c -> p (g j c)"), ih_rows[k]
                             ).then_inc(wih_loaded[k], 16)

            load_ih(0)
            wait(sp, consts_ready, 1)
            for row, b, gs in ((0, b_ih, ((0, 1), (1, 2), (2, 0))), (1, b_hh, ((0, 1), (1, 2), (2, 3)))):
                for g, region in gs:
                    r0 = row * 4 * K + region
                    sp.dma_start(bias32[r0:r0 + 4 * (K - 1) + 1:4, :],
                                 b[g * D:(g + 1) * D].rearrange("(j c) -> j c", c=P)).then_inc(bias_loaded, 16)
            load_ih(1)
            wait(sp, consts_ready, 2)
            for j in range(K):
                sp.dma_start(cond_sb[32 * j:32 * j + B, :], cond[:, j * P:(j + 1) * P]).then_inc(cond_loaded, 16)
            load_ih(2)
            load_x(0, 0)
            load_ih(3)
            wait(sp, bias_step, 5)
            wait(sp, consts_ready, 3)
            for n in range(3):
                for row in range(2):
                    r0, s0 = 2 * n + row, row * 4 * K
                    sp.dma_start(bias_rows[r0:r0 + 6 * (K - 1) + 1:6, :],
                                 bias_part[s0:s0 + 4 * K, n, :]).then_inc(bias_placed, 16)
            for k in range(K):
                sp.dma_start(rw32[:, k, :], router_w.rearrange("(j k c) e -> k j c e", j=K, k=K)[k]
                             ).then_inc(rw_loaded, 16)
            load_x(1, 1)
            wait(sp, weights_split, N_GRU_SPLITS)
            sp.dma_start(wb32, Wb.rearrange("e r n -> r e n")).then_inc(wb_loaded, 16)
            for k in range(K):
                for j in range(K):
                    d0 = j * P + k * 32
                    sp.dma_start(wa32[32 * j:32 * j + 32, k, :, :],
                                 Wa[:, d0:d0 + 32, :].rearrange("e p r -> p e r")).then_inc(wa_loaded, 16)
            with sp.Fori(1, NB - 1) as i:
                load_x(i + 1, i + 1)
                load_residual(i - 1)
                store(i - 1)
            load_x(0, NB)
            load_residual(NB - 2)
            store(NB - 2)
            load_residual(NB - 1)
            store(NB - 1)
            wait(sp, out_sent, 16 * NB)

        @block.gpsimd
        def _(pool):
            nc.gpsimd.memset(bias32[:, :], 0.0).then_inc(consts_ready, 1)
            nc.gpsimd.memset(cond_sb[:, :], 0.0).then_inc(consts_ready, 1)
            nc.gpsimd.memset(bias_rows[:, :], 0.0).then_inc(consts_ready, 1)
            nc.gpsimd.memset(bias_sel[:, :, :], PROD_SCALE).then_inc(consts_ready, 1)
            nc.gpsimd.memset(st[:, :, :, :, :], 0.0).then_inc(consts_ready, 1)
            nc.gpsimd.memset(ones[:, :], 1.0).then_inc(consts_ready, 1)
            nc.gpsimd.memset(half_pow[:, :], 0.5).then_inc(consts_ready, 1)
            pool.wait_ge(consts_ready, 7)
            nc.gpsimd.affine_select(out=bias_sel[:, :, :], in_=bias_sel[:, :, :], compare_op=ALU.is_ge, fill=0.0,
                                    base=0, pattern=[[-6, K], [0, 32]], channel_multiplier=1
                                    ).then_inc(consts_ready, 1)
            pool.wait_ge(consts_ready, 8)
            nc.gpsimd.affine_select(out=bias_sel[:, :, :], in_=bias_sel[:, :, :], compare_op=ALU.is_ge, fill=0.0,
                                    base=5, pattern=[[6, K], [0, 32]], channel_multiplier=-1
                                    ).then_inc(consts_ready, 1)
            nc.gpsimd.iota(expert_no[:, :], pattern=[[1, NE]], base=0, channel_multiplier=0,
                           allow_small_or_imprecise_dtypes=True).then_inc(consts_ready, 1)

            def square(f):
                wait(pool, h_ready, (f + 1) * S + 1)
                h = hist[:, :, :, :].rearrange("p k s b -> p (k s b)")
                nc.gpsimd.tensor_tensor(sq[:, :], h, h, ALU.mult).then_inc(sq_step, 1)
                wait(pool, sq_step, f * SQ_STEPS + 1)
                nc.gpsimd.tensor_tensor(sq2[:, :], sq[:, 0:2 * P], sq[:, 2 * P:4 * P], ALU.add).then_inc(sq_step, 1)
                wait(pool, sq_step, f * SQ_STEPS + 2)
                wait(pool, ssum_done, f)
                nc.gpsimd.tensor_tensor(sqs[:, :], sq2[:, 0:P], sq2[:, P:2 * P], ALU.add).then_inc(sq_step, 1)

            def root(f):
                wait(pool, router_read, 2 * (f + 1))
                nc.gpsimd.tensor_tensor(norm[:, :], ssum[:, :], half_pow[:, :], ALU.pow).then_inc(norm_ready, 1)

            with pool.Fori(1, NB + 1) as i:
                square(i - 1)
                root(i - 1)

        @block.scalar
        def _(act):
            for k in range(K):
                act.dma_start(whh32[:, k, :, :, :].rearrange("p g j c -> p (g j c)"),
                              W_hh.rearrange("(j k c) n -> k j c n", j=K, k=K)[k]).then_inc(whh_loaded[k], 16)

            def split_x(n):
                wait(act, x_turned, n + 1)
                wait(act, xpart_done, n * S // 2)
                nc.scalar.activation(xp[:, 0].rearrange("p r k c -> p (r k c)"),
                                     xt[:, :, :, :].rearrange("p r k c -> p (r k c)"), ACT.Copy,
                                     scale=PART_SCALE).then_inc(xhi_ready, 1)

            def gru_step(n, s):
                g = gates[s // 2 % 2]
                wait(act, gates_done, n + 1)
                nc.scalar.activation(rz[:, :], g[:, P:3 * P], ACT.Sigmoid, scale=1 / PROD_SCALE).then_inc(rz_ready, 1)
                wait(act, rz_ready, n + 1)
                nc.scalar.activation(omz[:, :], rz[:, P:2 * P], ACT.Copy, scale=-PART_SCALE,
                                     bias=PART_SCALE).then_inc(omz_ready, 1)
                wait(act, npre_ready, n + 1)
                nc.scalar.activation(nn[:, :], npre[:, :], ACT.Tanh, scale=1 / PROD_SCALE).then_inc(n_ready, 1)

            def split_states(f):
                wait(act, h_ready, (f + 1) * S + 1)
                wait(act, y_done, f * NE)
                nc.scalar.activation(hf[:, 0, :, :], hist[:, :, :, :].rearrange("p k s b -> p k (s b)"),
                                     ACT.Copy).then_inc(hfhi_ready, 1)

            def split_y(m, e):
                wait(act, y_done, m + 1)
                wait(act, o_done, m - 1 if e else m)
                nc.scalar.activation(y[:, e % 2, 0, :], ybank[e % 2][:, 0:P], ACT.Copy,
                                     scale=1 / PART_SCALE).then_inc(yhi_ready, 1)

            def weigh(f):
                wait(act, rnorm_step, (f + 1) * RN_STEPS)
                wait(act, top_step, (f + 1) * TOP_STEPS)
                nc.scalar.activation(wt[:, :], gap[:, :], ACT.Sigmoid, scale=rnorm[:, :]).then_inc(wt_ready, 1)

            def block_of(i, gru=True, ffn=True):
                for s in range(S):
                    if s == 0 and ffn:
                        split_states(i - 1)
                    if gru:
                        gru_step(i * S + s, s)
                        if s == 5:
                            split_x(i + 1)
                    if not ffn:
                        for n in LATE_SPLITS[s]:
                            split_weights(n)
                    if ffn:
                        if s <= 6:
                            split_y((i - 1) * NE + s, s)
                        if s == 1:
                            weigh(i - 1)
                        if s == 6:
                            split_y((i - 1) * NE + 7, 7)

            def split_weights(n):
                loaded, count, src, (hi, _) = SPLITS[n]
                wait(act, loaded, count)
                nc.scalar.activation(hi, src, ACT.Copy, scale=PART_SCALE).then_inc(hi_split, 1)

            for n in range(N_GRU_SPLITS):
                split_weights(n)
                if n == X_AFTER:
                    split_x(0)
            block_of(0, ffn=False)
            with act.Fori(1, NB) as i:
                block_of(i)
            block_of(NB, gru=False)

        @block.vector
        def _(dve):
            def turn_x(n):
                wait(dve, xin_loaded, N_XIN * (n + 1))
                wait(dve, xhi_ready, n)
                wait(dve, xlo_ready, n)
                nc.vector.transpose(xt[:, :, :, :].rearrange("p r k c -> p (r k c)"),
                                    xin[:, :, :].rearrange("p r c -> p (r c)")).then_inc(x_turned, 1)

            def split_x(n):
                wait(dve, xhi_ready, n + 1)
                nc.vector.scalar_tensor_tensor(out=xp[:, 1].rearrange("p r k c -> p (r k c)"),
                                               in0=xt[:, :, :, :].rearrange("p r k c -> p (r k c)"),
                                               scalar=PART_SCALE, in1=xp[:, 0].rearrange("p r k c -> p (r k c)"),
                                               op0=ALU.mult, op1=ALU.subtract).then_inc(xlo_ready, 1)

            def gru_step(n, s, i, ffn):
                g = gates[s // 2 % 2]
                q, q1 = s % 2, (s + 1) % 2
                wait(dve, rz_ready, n + 1)
                nc.vector.tensor_tensor(rhn[:, :], rz[:, 0:P], g[:, 3 * P:4 * P], ALU.mult).then_inc(rhn_ready, 1)
                wait(dve, rhn_ready, n + 1)
                nc.vector.tensor_tensor(npre[:, :], rhn[:, :], g[:, 0:P], ALU.add).then_inc(npre_ready, 1)
                nc.vector.transpose(zt[:, :, :].rearrange("p k c -> p (k c)"), rz[:, P:2 * P]).then_inc(z_turned, 1)
                wait(dve, z_turned, n + 1)
                nc.vector.tensor_tensor(v[:, :, :], zt[:, :, B * q:B * q + B], hist[:, :, (s - 1) % S, :],
                                        ALU.mult).then_inc(v_ready, 1)
                wait(dve, n_ready, n + 1)
                nc.vector.tensor_tensor(u[:, :], omz[:, :], nn[:, :], ALU.mult).then_inc(u_ready, 1)
                wait(dve, u_ready, n + 1)
                nc.vector.transpose(ut[:, :, :].rearrange("p k c -> p (k c)"), u[:, :]).then_inc(u_turned, 1)
                wait(dve, u_turned, n + 1)
                uTq = ut[:, :, B * q:B * q + B]
                nc.vector.tensor_tensor(st[:, q1, 0, :, B * q1:B * q1 + B], uTq, v[:, :, :],
                                        ALU.add).then_inc(hhi_ready, 1)
                if s == 0 and ffn:
                    wait(dve, hfhi_ready, i)
                    wait(dve, hflo_ready, i)
                    wait(dve, sq_step, (i - 1) * SQ_STEPS + 1)
                nc.vector.tensor_tensor(hist[:, :, s, :], uTq, v[:, :, :], ALU.add).then_inc(h_ready, 1)
                wait(dve, h_ready, n + 2)
                nc.vector.tensor_tensor(st[:, q1, 1, :, B * q1:B * q1 + B], hist[:, :, s, :],
                                        st[:, q1, 0, :, B * q1:B * q1 + B], ALU.subtract).then_inc(hlo_ready, 1)

            def split_states(f):
                wait(dve, hfhi_ready, f + 1)
                nc.vector.tensor_tensor(hf[:, 1, :, :], hist[:, :, :, :].rearrange("p k s b -> p k (s b)"),
                                        hf[:, 0, :, :], ALU.subtract).then_inc(hflo_ready, 1)

            def split_y(m, e):
                wait(dve, yhi_ready, m + 1)
                nc.vector.scalar_tensor_tensor(out=y[:, e % 2, 1, :], in0=ybank[e % 2][:, 0:P],
                                               scalar=1 / PART_SCALE, in1=y[:, e % 2, 0, :],
                                               op0=ALU.mult, op1=ALU.subtract).then_inc(ylo_ready, 1)

            def rank_experts(f):
                wait(dve, logits_done, f + 1)
                wait(dve, ssum_done, f + 1)
                nc.vector.tensor_copy(logit[:, :], rbank[:, 0:NE]).then_inc(router_read, 1)
                wait(dve, router_read, 2 * f + 1)
                nc.vector.tensor_copy(ssum[:, :], rbank[:, NE:NE + 1]).then_inc(router_read, 1)
                nc.vector.max(top[:, :], logit[:, :]).then_inc(top_step, 1)
                t0 = f * TOP_STEPS
                wait(dve, top_step, t0 + 1)
                nc.vector.tensor_tensor(gap[:, 0:1], top[:, 0:1], top[:, 1:2], ALU.subtract).then_inc(top_step, 1)
                nc.vector.tensor_tensor(gap[:, 1:2], top[:, 1:2], top[:, 0:1], ALU.subtract).then_inc(top_step, 1)
                nc.vector.max_index(top_at[:, :], top[:, :], logit[:, :]).then_inc(top_step, 1)
                wait(dve, top_step, t0 + 4)
                nc.vector.tensor_copy(top_no[:, :], top_at[:, :]).then_inc(top_step, 1)

            def invert_norm(f):
                r0 = f * RN_STEPS
                wait(dve, norm_ready, f + 1)
                nc.vector.tensor_scalar(normf[:, :], norm[:, :], NORM_FLOOR * PART_SCALE, PART_SCALE,
                                        ALU.max, ALU.mult).then_inc(rnorm_step, 1)
                wait(dve, rnorm_step, r0 + 1)
                nc.vector.reciprocal(rnorm[:, :], normf[:, :]).then_inc(rnorm_step, 1)

            def combine(f):
                c0 = f * COMB_STEPS
                wait(dve, wt_ready, f + 1)
                nc.vector.tensor_scalar(wts[:, :], wt[:, :], 1 / PROD_SCALE, None, ALU.mult).then_inc(comb_step, 1)
                wait(dve, top_step, (f + 1) * TOP_STEPS)
                wait(dve, comb_step, c0 + 1)
                for t in range(2):
                    nc.vector.tensor_scalar(pick[:, t, :], expert_no[:, :], top_no[:, t:t + 1], wts[:, t:t + 1],
                                            ALU.is_equal, ALU.mult).then_inc(comb_step, 1)
                wait(dve, comb_step, c0 + 3)
                nc.vector.tensor_tensor(comb[:, :], pick[:, 0, :], pick[:, 1, :], ALU.add).then_inc(comb_step, 1)

            def add_expert(f, e):
                m = f * NE + e
                bank = obank[e % 2]
                wait(dve, o_done, m + 1)
                if e == 0:
                    wait(dve, comb_step, (f + 1) * COMB_STEPS)
                    wait(dve, xres_loaded, 16 * (f + 1))
                if e == NE - 1:
                    wait(dve, out_sent, 16 * f)
                wait(dve, acc_done, m)
                nc.vector.scalar_tensor_tensor(out=(outb if e == NE - 1 else acc)[:, :], in0=bank[:, :],
                                               scalar=comb[:, e:e + 1], in1=(xres if e == 0 else acc)[:, :],
                                               op0=ALU.mult, op1=ALU.add).then_inc(acc_done, 1)

            def block_of(i, gru=True, ffn=True):
                f = i - 1
                for s in range(S):
                    if s == 0 and ffn:
                        split_states(f)
                    if gru:
                        gru_step(i * S + s, s, i, ffn)
                        if s == 4:
                            turn_x(i + 1)
                        if s == 5:
                            split_x(i + 1)
                    if not ffn:
                        for n in LATE_SPLITS[s]:
                            split_weights(n)
                    if ffn:
                        if s <= 6:
                            split_y(f * NE + s, s)
                        if s == 6:
                            split_y(f * NE + 7, 7)
                        if s == 0:
                            rank_experts(f)
                        if s == 1:
                            invert_norm(f)
                            combine(f)
                        if s >= 1:
                            add_expert(f, s - 1)
                        if s == 7:
                            add_expert(f, 7)

            def prepare_biases():
                dve.wait_ge(bias_loaded, 16 * 6)
                nc.vector.tensor_copy(bias_part[:, 0, :], bias32[:, :]).then_inc(bias_step, 1)
                dve.wait_ge(bias_step, 1)
                nc.vector.tensor_tensor(bias_rest[:, 0, :], bias32[:, :], bias_part[:, 0, :], ALU.subtract
                                        ).then_inc(bias_step, 1)
                dve.wait_ge(bias_step, 2)
                nc.vector.tensor_copy(bias_part[:, 1, :], bias_rest[:, 0, :]).then_inc(bias_step, 1)
                dve.wait_ge(bias_step, 3)
                nc.vector.tensor_tensor(bias_rest[:, 1, :], bias_rest[:, 0, :], bias_part[:, 1, :], ALU.subtract
                                        ).then_inc(bias_step, 1)
                dve.wait_ge(bias_step, 4)
                nc.vector.tensor_copy(bias_part[:, 2, :], bias_rest[:, 1, :]).then_inc(bias_step, 1)
            def prepare_state():
                dve.wait_ge(cond_loaded, 16 * K)
                nc.vector.transpose(cond_t[:, :, :].rearrange("p k c -> p (k c)"), cond_sb[:, :]).then_inc(cond_turned, 1)
                dve.wait_ge(cond_turned, 1)
                nc.vector.tensor_scalar(hist[:, :, S - 1, :], cond_t[:, :, 0:B], PART_SCALE, None, ALU.mult
                                        ).then_inc(h_ready, 1)
                dve.wait_ge(h_ready, 1)
                dve.wait_ge(consts_ready, 5)
                nc.vector.tensor_copy(st[:, 0, 0, :, 0:B], hist[:, :, S - 1, :]).then_inc(hhi_ready, 1)
                dve.wait_ge(hhi_ready, 1)
                nc.vector.tensor_tensor(st[:, 0, 1, :, 0:B], hist[:, :, S - 1, :], st[:, 0, 0, :, 0:B],
                                        ALU.subtract).then_inc(hlo_ready, 1)

            def split_weights(n):
                _, _, src, (hi, lo) = SPLITS[n]
                wait(dve, hi_split, n + 1)
                nc.vector.scalar_tensor_tensor(out=lo, in0=src, scalar=PART_SCALE, in1=hi, op0=ALU.mult,
                                               op1=ALU.subtract).then_inc(weights_split, 1)

            for n in range(N_GRU_SPLITS):
                if n == BIAS_AT:
                    prepare_biases()
                if n == STATE_AT:
                    prepare_state()
                split_weights(n)
                if n == X_AFTER - 2:
                    turn_x(0)
                if n == X_AFTER:
                    split_x(0)
            block_of(0, ffn=False)
            with dve.Fori(1, NB) as i:
                block_of(i)
            block_of(NB, gru=False)

        @block.tensor
        def _(pe):
            def x_half(pair, half, blk):
                g = gates[pair % 2]
                if half == 0:
                    if pair % (S // 2) == 0:
                        wait(pe, xhi_ready, blk + 1)
                        wait(pe, xlo_ready, blk + 1)
                    nc.tensor.matmul(g[:, :], bias_sel[:, :, :].rearrange("p j c -> p (j c)"), bias_rows[:, :],
                                     start=True, stop=False, skip_group_check=True)
                r = pair % (S // 2)
                for k in range(2 * half, 2 * half + 2):
                    for ph, pw in TERMS:
                        for j in range(K):
                            mm = nc.tensor.matmul(g[32 * j:32 * j + 32, 0:G], xp[:, ph, r, k, :],
                                                  wih[:, pw, k, j, :], start=False, stop=False,
                                                  skip_group_check=True)
                if half == 1:
                    mm.then_inc(xpart_done, 1)

            def state_part(n, s):
                g = gates[s // 2 % 2]
                for ph, pw in TERMS:
                    if pw == 0:
                        wait(pe, (hhi_ready, hlo_ready)[ph], n + 1)
                    for k in range(K):
                        for j in range(K):
                            mm = nc.tensor.matmul(g[32 * j:32 * j + 32, P:4 * P], st[:, s % 2, ph, k, :],
                                                  whh[:, pw, k, j, :], start=False, stop=True,
                                                  skip_group_check=True)
                mm.then_inc(gates_done, 1)

            def logits(f):
                wait(pe, hfhi_ready, f + 1)
                wait(pe, hflo_ready, f + 1)
                wait(pe, router_read, 2 * f)
                n = 0
                for k in range(K):
                    for ph, pw in TERMS:
                        mm = nc.tensor.matmul(rbank[:, 0:NE], hf[:, ph, k, :], rw[:, pw, k, :], start=(n == 0),
                                              stop=(n == 3 * K - 1), skip_group_check=True)
                        n += 1
                mm.then_inc(logits_done, 1)

            def sum_squares(f):
                wait(pe, sq_step, (f + 1) * SQ_STEPS)
                nc.tensor.matmul(rbank[:, NE:NE + 1], sqs[:, :], ones[:, :], start=False, stop=True,
                                 skip_group_check=True).then_inc(ssum_done, 1)

            def expert_down(f, e):
                m = f * NE + e
                wait(pe, ylo_ready, m - 1 if e else m)
                n = 0
                for k in range(K):
                    for ph, pw in TERMS:
                        mm = nc.tensor.matmul(ybank[e % 2][:, 0:P], wa[:, pw, k, e, :], hf[:, ph, k, :],
                                              start=(n == 0), stop=(n == 3 * K - 1))
                        n += 1
                mm.then_inc(y_done, 1)

            def expert_up(f, e):
                m = f * NE + e
                bank = obank[e % 2]
                wait(pe, ylo_ready, m + 1)
                wait(pe, acc_done, m - 1 if e else m)
                for n, (ph, pw) in enumerate(TERMS):
                    mm = nc.tensor.matmul(bank[:, :], y[:, e % 2, ph, :], wb[:, pw, e, :], start=(n == 0),
                                          stop=(n == 2))
                mm.then_inc(o_done, 1)

            def block_of(i, gru=True, ffn=True):
                f = i - 1
                for s in range(S):
                    n = i * S + s
                    if gru:
                        state_part(n, s)
                    if ffn:
                        if s == 0:
                            logits(f)
                        if s <= 6:
                            expert_down(f, s)
                        if s == 6:
                            expert_down(f, 7)
                        if s == 7:
                            expert_up(f, 6)
                    if gru:
                        x_half(s // 2 + 1, s % 2, i + 1)
                    if ffn:
                        if s == 0:
                            sum_squares(f)
                        if 1 <= s <= 6:
                            expert_up(f, s - 1)
                        if s == 7:
                            expert_up(f, 7)

            pe.wait_ge(consts_ready, N_CONST + 2)
            pe.wait_ge(bias_placed, 16 * 6)
            pe.wait_ge(weights_split, N_GRU_SPLITS - 3)
            x_half(0, 0, 0)
            pe.wait_ge(weights_split, N_GRU_SPLITS)
            x_half(0, 1, 0)
            block_of(0, ffn=False)
            pe.wait_ge(weights_split, len(SPLITS))
            with pe.Fori(1, NB) as i:
                block_of(i)
            block_of(NB, gru=False)


_INS = ['x', 'cond_2048', 'L0_cond_W_ih', 'L0_cond_W_hh', 'L0_cond_b_ih', 'L0_cond_b_hh', 'L0_ffn_router_w',
        'L0_ffn_Wa', 'L0_ffn_Wb']


def kernel(**inputs):
    import numpy as np
    import concourse.bacc as bacc
    from concourse.bass_utils import run_bass_kernel_spmd

    nc = bacc.Bacc("TRN2", target_bir_lowering=False, num_devices=1)
    arrays, args = {}, []
    for name in _INS:
        a = np.ascontiguousarray(inputs[name])
        arrays[f"in_{name}"] = a
        args.append(nc.dram_tensor(f"in_{name}", a.shape, mybir.dt.from_np(a.dtype), kind="ExternalInput").ap())
    shape = inputs['x'].shape
    args.append(nc.dram_tensor("out_0", shape, F32, kind="ExternalOutput").ap())
    gru_moe_kernel(nc, *args)
    return run_bass_kernel_spmd(nc, [arrays], core_ids=[0]).results[0]["out_0"]
```

```python
from contextlib import ExitStack

import concourse.bass as bass
from concourse import mybir

F32 = mybir.dt.float32
F16 = mybir.dt.float16
U32 = mybir.dt.uint32
ALU = mybir.AluOpType
ACT = mybir.ActivationFunctionType

P = 128
PART_SCALE = 128.0
PROD_SCALE = PART_SCALE * PART_SCALE
TERMS = ((0, 0), (0, 1), (1, 0))
NORM_FLOOR = 1e-12


def wait(eng, sem, value):
    if isinstance(value, int) and value <= 0:
        return
    eng.wait_ge(sem, value)


def gru_moe_kernel(nc, x, cond, W_ih, W_hh, b_ih, b_hh, router_w, Wa, Wb, out):
    B, T, D = x.shape
    NE, _, R = Wa.shape
    K = D // P
    S = P // B
    NB = T // S
    G = 3 * P
    assert B * 2 == 32 and R == P and D == K * P and K == 4 and NE == S == 8

    x_blocks = x.rearrange("b (n t) d -> n t b d", t=S)
    x_parts = x.rearrange("b (n r q) (j c) -> n j q b r c", q=2, r=S // 2, j=K)
    out_blocks = out.rearrange("b (n t) d -> n t b d", t=S)

    with ExitStack() as ctx:
        def sb(name, shape, dt=F32):
            return ctx.enter_context(nc.sbuf_tensor(name, shape, dt))

        def ps(name, shape):
            return ctx.enter_context(nc.psum_tensor(name, shape, F32))

        def sem(name):
            return ctx.enter_context(nc.semaphore(name))

        whh32 = sb("whh32", [P, K, 3, K, P])
        wih32 = sb("wih32", [P, K, 3, K, P])
        wa32 = wih32[:, :, :, :, :].rearrange("p k g j c -> p (k g j c)")[:, 0:K * NE * R].rearrange(
            "p (k e r) -> p k e r", k=K, e=NE)
        wb32 = whh32[:, :, :, :, :].rearrange("p k g j c -> p (k g j c)")[:, 0:NE * D].rearrange(
            "p (e n) -> p e n", e=NE)
        rw32 = sb("rw32", [P, K, NE])
        whh = sb("whh", [P, 2, K, K, G], F16)
        wih = sb("wih", [P, 2, K, 3, D], F16)
        wa = sb("wa", [P, 2, K, NE, R], F16)
        wb = sb("wb", [P, 2, NE, D], F16)
        rw = sb("rw", [P, 2, K, NE], F16)
        bias_rows = sb("bias_rows", [2, 3, D])
        scale_rows = sb("scale_rows", [2, P])
        bias_in = sb("bias_in", [P, 3, D])
        bias_hn = sb("bias_hn", [P, P])
        hn_p = sb("hn_p", [P, 2, P], F16)
        ident = sb("ident", [P, K, 2, B], F16)
        cross = sb("cross", [P, 2, K, 2, B], F16)
        ones = sb("ones", [P, 1])
        half_pow = sb("half_pow", [P, 1])
        table_use = sb("table_use", [P, 1])
        expert_no = sb("expert_no", [P, NE])
        cond_sb = sb("cond_sb", [P, P])
        cond_t = sb("cond_t", [P, K, 32])
        xin = sb("xin", [P, S // 2, P])
        xt = sb("xt", [P, K, S // 2, 32])
        xp = sb("xp", [P, 2, K, P], F16)
        gi32 = sb("gi32", [P, 3, D])
        gi_p = sb("gi_p", [P, 2, 2, K, 3, P], F16)
        st = sb("st", [P, 2, 2, K, 32], F16)
        low_sum = sb("low_sum", [P, G], F16)
        high = sb("high", [P, G])
        hist = sb("hist", [P, K, S, B])
        pre = sb("pre", [P, 3, P])
        rr = sb("rr", [P, P])
        zz = sb("zz", [P, P])
        omzt = sb("omzt", [P, K, B])
        rhn = sb("rhn", [P, P])
        npre = sb("npre", [P, P])
        nn = sb("nn", [P, P])
        u = sb("u", [P, K, B])
        zt = sb("zt", [P, K, 32])
        nt = sb("nt", [P, K, 32])
        v = sb("v", [P, K, B])
        hf = sb("hf", [P, 2, K, P], F16)
        sq = sb("sq", [P, K * P])
        sq2 = sb("sq2", [P, 2 * P])
        sqs = sb("sqs", [P, P])
        logit = sb("logit", [P, NE])
        ssum = sb("ssum", [P, 1])
        norm = sb("norm", [P, 1])
        normf = sb("normf", [P, 1])
        rnorm = sb("rnorm", [P, 1])
        top = sb("top", [P, 8])
        top_at = sb("top_at", [P, 8], U32)
        top_no = sb("top_no", [P, 8])
        gap = sb("gap", [P, 2])
        wt = sb("wt", [P, 2])
        wts = sb("wts", [P, 2])
        pick = sb("pick", [P, 2, NE])
        comb = sb("comb", [P, NE])
        y = sb("y", [P, 2, 2, P], F16)
        xres = sb("xres", [P, D])
        acc = sb("acc", [P, D])
        outb = sb("outb", [P, D])
        gates = [ps(f"gates{i}", [P, 4 * P]) for i in range(2)]
        ybank = [ps(f"ybank{i}", [P, 4 * P]) for i in range(2)]
        obank = [ps(f"obank{i}", [P, 4 * P]) for i in range(2)]
        high_sum = ps("high_sum", [P, 4 * P])
        rbank = obank[1]
        gibank = ps("gibank", [P, 4 * P])

        first_gi = [obank[0], obank[1], gibank]

        consts_ready = sem("consts_ready")
        cond_loaded = sem("cond_loaded")
        bias_loaded = sem("bias_loaded")
        hn_bias_loaded = sem("hn_bias_loaded")
        whh_loaded = [sem(f"whh{k}_loaded") for k in range(K)]
        wih_loaded = [sem(f"wih{k}_loaded") for k in range(K)]
        wa_loaded, wb_loaded, rw_loaded = sem("wa_loaded"), sem("wb_loaded"), sem("rw_loaded")
        hi_split = sem("hi_split")
        weights_split = sem("weights_split")
        hn_bias_step = sem("hn_bias_step")
        bias_spread = sem("bias_spread")
        bias_copied = sem("bias_copied")
        xin_loaded = sem("xin_loaded")
        cond_turned = sem("cond_turned")
        x_turned = sem("x_turned")
        xhi_ready = sem("xhi_ready")
        xlo_ready = sem("xlo_ready")
        gi_done = sem("gi_done")
        gi_biased = sem("gi_biased")
        gi_hi_ready = sem("gi_hi_ready")
        gi_lo_ready = sem("gi_lo_ready")
        seeds_done = sem("seeds_done")
        r_summed = sem("r_summed")
        hn_summed = sem("hn_summed")
        z_summed = sem("z_summed")
        sums_ready = sem("sums_ready")
        r_ready = sem("r_ready")
        z_ready = sem("z_ready")
        rhn_ready = sem("rhn_ready")
        npre_ready = sem("npre_ready")
        n_ready = sem("n_ready")
        z_turned = sem("z_turned")
        u_ready = sem("u_ready")
        n_turned = sem("n_turned")
        hhi_ready = sem("hhi_ready")
        h_ready = sem("h_ready")
        both_parts_ready = sem("both_parts_ready")
        products_done = sem("products_done")
        low_copied = sem("low_copied")
        hfhi_ready = sem("hfhi_ready")
        hflo_ready = sem("hflo_ready")
        sq_step = sem("sq_step")
        logits_done = sem("logits_done")
        ssum_done = sem("ssum_done")
        router_read = sem("router_read")
        top_step = sem("top_step")
        norm_ready = sem("norm_ready")
        rnorm_step = sem("rnorm_step")
        wt_ready = sem("wt_ready")
        comb_step = sem("comb_step")
        y_done = sem("y_done")
        yhi_ready = sem("yhi_ready")
        ylo_ready = sem("ylo_ready")
        o_done = sem("o_done")
        acc_done = sem("acc_done")
        xres_loaded = sem("xres_loaded")
        out_sent = sem("out_sent")

        N_MEMSETS, N_CONST = 8, 12
        SQ_STEPS, TOP_STEPS, RN_STEPS, COMB_STEPS = 3, 5, 2, 4
        N_XIN = 16 * 2 * K
        SPLITS = []

        def split_ih(k):
            for g in range(3):
                SPLITS.append((wih_loaded[k], 16, wih32[:, k, g, :, :].rearrange("p j c -> p (j c)"),
                               [wih[:, p, k, g, :] for p in range(2)]))

        def split_hh(k):
            for g in range(3):
                SPLITS.append((whh_loaded[k], 16, whh32[:, k, g, :, :],
                               [whh[:, p, k, :, g * P:(g + 1) * P] for p in range(2)]))

        IH_ORDER = (1, 3, 0, 2)
        split_ih(1)
        split_ih(3)
        split_hh(0)
        split_ih(0)
        split_ih(2)
        for k in range(1, K):
            split_hh(k)
        IH_SPLIT = (3, 6, 12, 15)
        WA_FREE, WB_FREE = 15, 21
        N_GRU_SPLITS = len(SPLITS)
        BIAS_AT, TURN_X0_AT, SPLIT_X0_AT, STATE_AT = 11, 12, 12, 18
        SPLITS.append((rw_loaded, 16 * K, rw32[:, :, :], [rw[:, p, :, :] for p in range(2)]))
        for e in range(0, NE, 2):
            SPLITS.append((wb_loaded, 16, wb32[:, e:e + 2, :], [wb[:, p, e:e + 2, :] for p in range(2)]))
        for k in range(K):
            SPLITS.append((wa_loaded, 16 * K * K, wa32[:, k, :, :], [wa[:, p, k, :, :] for p in range(2)]))

        LATE_SPLITS = [[N_GRU_SPLITS + n for n in ns] for ns in ([], [0], [1], [2], [3, 4], [5, 6], [7, 8], [])]

        PER_GATE = K * len(TERMS)
        GI_GATES = (2, 0, 1)
        GI_WORK = ((1, 7, 12), (1, 12, 17), (1, 17, 21), (1, 21, 24), (1, 24, 29), (1, 29, 36), (2, 0, 3), (2, 3, 7))
        SEED_WORK = {0: 1, 3: 2, 4: 3, 7: 4}
        BIAS_WORK = {0: (0,), 3: (1,), 5: (2,)}
        SPLIT_WORK = {1: (0,), 4: (1,), 6: (2,)}
        TURN_X_AT, SPLIT_X_AT = 1, 5
        ADD_WORK = ((), (), (0,), (1,), (2, 3), (4,), (5,), (6, 7))

        block = ctx.enter_context(nc.Block())

        @block.sync
        def _(sp):
            def load_x(blk, n):
                wait(sp, x_turned, n)
                for j in range(K):
                    for q in range(2):
                        p0 = 32 * j + B * q
                        sp.dma_start(xin[p0:p0 + B, :, :], x_parts[blk, j, q]).then_inc(xin_loaded, 16)

            def load_residual(f):
                wait(sp, acc_done, f * NE)
                sp.dma_start(xres[:, :], x_blocks[f]).then_inc(xres_loaded, 16)

            def store(f):
                sp.wait_ge(acc_done, (f + 1) * NE)
                sp.dma_start(out_blocks[f], outb[:, :]).then_inc(out_sent, 16)

            ih_rows = W_ih.rearrange("(j k c) n -> k j c n", j=K, k=K)

            def load_ih(k):
                sp.dma_start(wih32[:, k, :, :, :].rearrange("p g j c -> p (g j c)"), ih_rows[k]
                             ).then_inc(wih_loaded[k], 16)

            def load_hh(k):
                sp.dma_start(whh32[:, k, :, :, :].rearrange("p g j c -> p (g j c)"),
                             W_hh.rearrange("(j k c) n -> k j c n", j=K, k=K)[k]).then_inc(whh_loaded[k], 16)

            sp.wait_ge(consts_ready, 1)
            sp.dma_start(bias_rows[0:1, :, :].rearrange("p g n -> p (g n)"), b_ih.rearrange("(p n) -> p n", p=1)
                         ).then_inc(bias_loaded, 16)
            sp.dma_start(bias_rows[1:2, 0:2, :].rearrange("p g n -> p (g n)"),
                         b_hh[0:2 * D].rearrange("(p n) -> p n", p=1)).then_inc(bias_loaded, 16)
            load_ih(0)
            load_x(0, 0)
            load_ih(2)
            sp.wait_ge(consts_ready, 2)
            for j in range(K):
                sp.dma_start(cond_sb[32 * j:32 * j + B, :], cond[:, j * P:(j + 1) * P]).then_inc(cond_loaded, 16)
            load_hh(1)
            load_hh(2)
            for j in range(K):
                c0 = 2 * D + j * P
                sp.dma_start(bias_hn[32 * j:32 * j + 32, :], b_hh[c0:c0 + P].partition_broadcast(32)
                             ).then_inc(hn_bias_loaded, 16)
            load_hh(3)
            for k in range(K):
                sp.dma_start(rw32[:, k, :], router_w.rearrange("(j k c) e -> k j c e", j=K, k=K)[k]
                             ).then_inc(rw_loaded, 16)
            load_x(1, 1)
            sp.wait_ge(weights_split, WA_FREE)
            for k in range(K):
                for j in range(K):
                    d0 = j * P + k * 32
                    sp.dma_start(wa32[32 * j:32 * j + 32, k, :, :],
                                 Wa[:, d0:d0 + 32, :].rearrange("e p r -> p e r")).then_inc(wa_loaded, 16)
            sp.wait_ge(weights_split, WB_FREE)
            sp.dma_start(wb32, Wb.rearrange("e r n -> r e n")).then_inc(wb_loaded, 16)
            load_x(2, 2)
            load_x(3, 3)
            with sp.Fori(1, NB - 3) as i:
                load_residual(i - 1)
                load_x(i + 3, i + 3)
                store(i - 1)
            for i in range(NB - 3, NB + 1):
                load_residual(i - 1)
                if i < NB - 1:
                    load_x(0, i + 3)
                store(i - 1)
            sp.wait_ge(out_sent, 16 * NB)
            sp.wait_ge(xin_loaded, N_XIN * (NB + 2))

        @block.gpsimd
        def _(pool):
            nc.gpsimd.memset(bias_rows[:, 2, :], 0.0).then_inc(consts_ready, 1)
            nc.gpsimd.memset(cond_sb[:, :], 0.0).then_inc(consts_ready, 1)
            nc.gpsimd.memset(st[:, :, :, :, :], 0.0).then_inc(consts_ready, 1)
            nc.gpsimd.memset(ident[:, :, :, :], 0.0).then_inc(consts_ready, 1)
            nc.gpsimd.memset(ones[:, :], 1.0).then_inc(consts_ready, 1)
            nc.gpsimd.memset(half_pow[:, :], 0.5).then_inc(consts_ready, 1)
            nc.gpsimd.memset(scale_rows[:, :], PROD_SCALE).then_inc(consts_ready, 1)
            nc.gpsimd.memset(cross[:, :, :, :, :], 0.0).then_inc(consts_ready, 1)
            pool.wait_ge(consts_ready, 4)
            diagonal = ident[:, :, :, :].rearrange("p j q b -> p (j q b)")
            nc.gpsimd.affine_select(out=diagonal, in_=diagonal, compare_op=ALU.not_equal, fill=PART_SCALE,
                                    base=0, pattern=[[-1, P]], channel_multiplier=1).then_inc(consts_ready, 1)
            nc.gpsimd.iota(expert_no[:, :], pattern=[[1, NE]], base=0, channel_multiplier=0,
                           allow_small_or_imprecise_dtypes=True).then_inc(consts_ready, 1)
            pool.wait_ge(consts_ready, N_MEMSETS + 1)
            for q in range(2):
                nc.gpsimd.tensor_copy(cross[:, q, :, q, :], ident[:, :, 1 - q, :]).then_inc(consts_ready, 1)

            def square(f):
                pool.wait_ge(h_ready, (f + 1) * S + 1)
                h = hist[:, :, :, :].rearrange("p k s b -> p (k s b)")
                nc.gpsimd.tensor_tensor(sq[:, :], h, h, ALU.mult).then_inc(sq_step, 1)
                pool.wait_ge(sq_step, f * SQ_STEPS + 1)
                nc.gpsimd.tensor_tensor(sq2[:, :], sq[:, 0:2 * P], sq[:, 2 * P:4 * P], ALU.add).then_inc(sq_step, 1)
                pool.wait_ge(sq_step, f * SQ_STEPS + 2)
                wait(pool, ssum_done, f)
                nc.gpsimd.tensor_tensor(sqs[:, :], sq2[:, 0:P], sq2[:, P:2 * P], ALU.add).then_inc(sq_step, 1)

            def root(f):
                pool.wait_ge(router_read, 2 * (f + 1))
                nc.gpsimd.tensor_tensor(norm[:, :], ssum[:, :], half_pow[:, :], ALU.pow).then_inc(norm_ready, 1)

            def split_gates(b, parity):
                for c in range(3):
                    pool.wait_ge(gi_hi_ready, 3 * b + c + 1)
                    nc.gpsimd.tensor_tensor(gi_p[:, parity, 1, :, c, :],
                                            gi32[:, c, :].rearrange("p (j c) -> p j c", c=P),
                                            gi_p[:, parity, 0, :, c, :], ALU.subtract).then_inc(gi_lo_ready, 1)

            def block_of(i, parity):
                square(i - 1)
                root(i - 1)
                split_gates(i + 1, 1 - parity)

            split_gates(1, 1)
            with pool.Fori(0, NB // 2 - 1) as t:
                block_of(t * 2 + 1, 1)
                block_of(t * 2 + 2, 0)
            block_of(NB - 1, 1)
            square(NB - 1)
            root(NB - 1)

        @block.scalar
        def _(act):
            for k in (1, 3):
                act.dma_start(wih32[:, k, :, :, :].rearrange("p g j c -> p (g j c)"),
                              W_ih.rearrange("(j k c) n -> k j c n", j=K, k=K)[k]).then_inc(wih_loaded[k], 16)
            act.dma_start(whh32[:, 0, :, :, :].rearrange("p g j c -> p (g j c)"),
                          W_hh.rearrange("(j k c) n -> k j c n", j=K, k=K)[0]).then_inc(whh_loaded[0], 16)

            def split_x(n):
                act.wait_ge(x_turned, n + 1)
                wait(act, gi_done, 3 * n)
                nc.scalar.activation(xp[:, 0, :, :].rearrange("p k c -> p (k c)"),
                                     xt[:, :, :, :].rearrange("p k r c -> p (k r c)"), ACT.Copy,
                                     scale=PART_SCALE).then_inc(xhi_ready, 1)

            def gru_step(n, s):
                act.wait_ge(products_done, n + 1)
                nc.scalar.activation(low_sum[:, :], high_sum[:, 0:G], ACT.Copy, scale=1 / PART_SCALE
                                     ).then_inc(low_copied, 1)
                nc.scalar.activation(high[:, :], high_sum[:, 0:G], ACT.Copy).then_inc(sums_ready, 1)
                act.wait_ge(r_summed, n + 1)
                nc.scalar.activation(rr[:, :], pre[:, 0, :], ACT.Sigmoid, scale=1 / PROD_SCALE).then_inc(r_ready, 1)
                act.wait_ge(z_summed, n + 1)
                nc.scalar.activation(zz[:, :], pre[:, 1, :], ACT.Sigmoid, scale=1 / PROD_SCALE).then_inc(z_ready, 1)
                act.wait_ge(npre_ready, n + 1)
                nc.scalar.activation(nn[:, :], npre[:, :], ACT.Tanh, scale=1 / PROD_SCALE).then_inc(n_ready, 1)

            def copy_high(n, q):
                act.wait_ge(hhi_ready, n + 1)
                nc.scalar.activation(st[:, q, 1, :, B * q:B * q + B], st[:, q, 0, :, B * q:B * q + B], ACT.Copy
                                     ).then_inc(both_parts_ready, 1)

            def split_gates(b, c, own_parity):
                act.wait_ge(gi_biased, 3 * (b - 1) + c + 1)
                wait(act, seeds_done, (b - 1) * (S // 2))
                nc.scalar.activation(gi_p[:, own_parity, 0, :, c, :], gi32[:, c, :].rearrange("p (j c) -> p j c", c=P),
                                     ACT.Copy).then_inc(gi_hi_ready, 1)

            def split_states(f):
                act.wait_ge(h_ready, (f + 1) * S + 1)
                wait(act, y_done, f * NE)
                nc.scalar.activation(hf[:, 0, :, :], hist[:, :, :, :].rearrange("p k s b -> p k (s b)"),
                                     ACT.Copy).then_inc(hfhi_ready, 1)

            def split_y(m, e):
                act.wait_ge(y_done, m + 1)
                wait(act, o_done, m - 1 if e else m)
                nc.scalar.activation(y[:, e % 2, 0, :], ybank[e % 2][:, 0:P], ACT.Copy,
                                     scale=1 / PART_SCALE).then_inc(yhi_ready, 1)

            def weigh(f):
                act.wait_ge(rnorm_step, (f + 1) * RN_STEPS)
                act.wait_ge(top_step, (f + 1) * TOP_STEPS)
                nc.scalar.activation(wt[:, :], gap[:, :], ACT.Sigmoid, scale=rnorm[:, :]).then_inc(wt_ready, 1)

            def block_of(i, parity, gru=True, ffn=True):
                for s in range(S):
                    if s == 0 and ffn:
                        split_states(i - 1)
                    if gru:
                        gru_step(i * S + s, s)
                        copy_high(i * S + s + 1, (s + 1) % 2)
                        for c in SPLIT_WORK.get(s, ()):
                            split_gates(i + 1, c, 1 - parity)
                        if s == SPLIT_X_AT:
                            split_x(i + 2)
                    if not ffn:
                        for n in LATE_SPLITS[s]:
                            split_weights(n)
                    if ffn:
                        if s == 2:
                            weigh(i - 1)
                        if s <= 6:
                            split_y((i - 1) * NE + s, s)
                        if s == 6:
                            split_y((i - 1) * NE + 7, 7)

            def split_weights(n):
                loaded, count, src, (hi, _) = SPLITS[n]
                wait(act, loaded, count)
                nc.scalar.activation(hi, src, ACT.Copy, scale=PART_SCALE).then_inc(hi_split, 1)

            act.wait_ge(consts_ready, 5)
            nc.scalar.activation(table_use[:, :], ones[:, :], ACT.Sigmoid)
            for n in range(N_GRU_SPLITS):
                if n == BIAS_AT:
                    for c in range(3):
                        act.wait_ge(bias_spread, c + 1)
                        nc.scalar.activation(bias_in[:, c, :], first_gi[c][:, :], ACT.Copy, scale=1 / PART_SCALE
                                             ).then_inc(bias_copied, 1)
                if n == SPLIT_X0_AT:
                    split_x(0)
                split_weights(n)
            for c in range(3):
                act.wait_ge(gi_done, c + 1)
                nc.scalar.activation(gi_p[:, 0, 0, :, c, :], first_gi[c][:, :].rearrange("p (j c) -> p j c", c=P),
                                     ACT.Copy, scale=1 / PART_SCALE).then_inc(gi_hi_ready, 1)
            copy_high(0, 0)
            split_x(1)
            block_of(0, 0, ffn=False)
            with act.Fori(0, NB // 2 - 1) as t:
                block_of(t * 2 + 1, 1)
                block_of(t * 2 + 2, 0)
            block_of(NB - 1, 1)
            block_of(NB, 0, gru=False)

        @block.vector
        def _(dve):
            def turn_x(n):
                dve.wait_ge(xin_loaded, N_XIN * (n + 1))
                wait(dve, xhi_ready, n)
                wait(dve, xlo_ready, n)
                nc.vector.transpose(xt[:, :, :, :].rearrange("p k r c -> p r k c"),
                                    xin[:, :, :].rearrange("p r (k c) -> p r k c", c=32)).then_inc(x_turned, 1)

            def split_x(n):
                dve.wait_ge(xhi_ready, n + 1)
                nc.vector.scalar_tensor_tensor(out=xp[:, 1, :, :].rearrange("p k c -> p (k c)"),
                                               in0=xt[:, :, :, :].rearrange("p k r c -> p (k r c)"),
                                               scalar=PART_SCALE, in1=xp[:, 0, :, :].rearrange("p k c -> p (k c)"),
                                               op0=ALU.mult, op1=ALU.subtract).then_inc(xlo_ready, 1)

            def bias_gate(b, c):
                dve.wait_ge(gi_done, 3 * b + c + 1)
                wait(dve, gi_lo_ready, 3 * b + c - 2)
                nc.vector.scalar_tensor_tensor(out=gi32[:, c, :], in0=gibank[:, :], scalar=1 / PART_SCALE,
                                               in1=bias_in[:, c, :], op0=ALU.mult, op1=ALU.add
                                               ).then_inc(gi_biased, 1)

            def gru_step(n, s, i, ffn):
                g = gates[s // 2 % 2]
                q, q1 = s % 2, (s + 1) % 2
                dve.wait_ge(sums_ready, 2 * (n + 1))
                nc.vector.tensor_tensor(pre[:, 0, :], g[:, P:2 * P], high[:, 0:P], ALU.add).then_inc(r_summed, 1)
                nc.vector.tensor_tensor(pre[:, 2, :], g[:, 3 * P:4 * P], high[:, 2 * P:3 * P], ALU.add
                                        ).then_inc(hn_summed, 1)
                nc.vector.tensor_tensor(pre[:, 1, :], g[:, 2 * P:3 * P], high[:, P:2 * P], ALU.add
                                        ).then_inc(z_summed, 1)
                dve.wait_ge(r_ready, n + 1)
                dve.wait_ge(hn_summed, n + 1)
                nc.vector.tensor_tensor(rhn[:, :], rr[:, :], pre[:, 2, :], ALU.mult).then_inc(rhn_ready, 1)
                dve.wait_ge(rhn_ready, n + 1)
                nc.vector.tensor_tensor(npre[:, :], rhn[:, :], g[:, 0:P], ALU.add).then_inc(npre_ready, 1)
                dve.wait_ge(z_ready, n + 1)
                nc.vector.transpose(zt[:, :, :].rearrange("p k c -> p (k c)"), zz[:, :]).then_inc(z_turned, 1)
                dve.wait_ge(z_turned, n + 1)
                nc.vector.tensor_scalar(omzt[:, :, :], zt[:, :, B * q:B * q + B], -PART_SCALE, PART_SCALE, ALU.mult,
                                        ALU.add)
                dve.wait_ge(n_ready, n + 1)
                nc.vector.transpose(nt[:, :, :].rearrange("p k c -> p (k c)"), nn[:, :]).then_inc(n_turned, 1)
                nc.vector.tensor_tensor(v[:, :, :], zt[:, :, B * q:B * q + B], hist[:, :, (s - 1) % S, :],
                                        ALU.mult)
                dve.wait_ge(n_turned, n + 1)
                nc.vector.tensor_tensor(u[:, :, :], nt[:, :, B * q:B * q + B], omzt[:, :, :], ALU.mult
                                        ).then_inc(u_ready, 1)
                dve.wait_ge(u_ready, n + 1)
                nc.vector.tensor_tensor(st[:, q1, 0, :, B * q1:B * q1 + B], u[:, :, :], v[:, :, :],
                                        ALU.add).then_inc(hhi_ready, 1)
                if s == 0 and ffn:
                    wait(dve, hfhi_ready, i)
                    wait(dve, hflo_ready, i)
                    wait(dve, sq_step, (i - 1) * SQ_STEPS + 1)
                nc.vector.tensor_tensor(hist[:, :, s, :], u[:, :, :], v[:, :, :], ALU.add).then_inc(h_ready, 1)
                dve.wait_ge(h_ready, n + 2)
                nc.vector.tensor_tensor(st[:, q1, 1, :, B * q:B * q + B], hist[:, :, s, :],
                                        st[:, q1, 0, :, B * q1:B * q1 + B], ALU.subtract).then_inc(both_parts_ready, 1)

            def split_states(f):
                dve.wait_ge(hfhi_ready, f + 1)
                nc.vector.tensor_tensor(hf[:, 1, :, :], hist[:, :, :, :].rearrange("p k s b -> p k (s b)"),
                                        hf[:, 0, :, :], ALU.subtract).then_inc(hflo_ready, 1)

            def split_y(m, e):
                dve.wait_ge(yhi_ready, m + 1)
                nc.vector.scalar_tensor_tensor(out=y[:, e % 2, 1, :], in0=ybank[e % 2][:, 0:P],
                                               scalar=1 / PART_SCALE, in1=y[:, e % 2, 0, :],
                                               op0=ALU.mult, op1=ALU.subtract).then_inc(ylo_ready, 1)

            def rank_experts(f):
                dve.wait_ge(logits_done, f + 1)
                dve.wait_ge(ssum_done, f + 1)
                nc.vector.tensor_copy(logit[:, :], rbank[:, 0:NE]).then_inc(router_read, 1)
                dve.wait_ge(router_read, 2 * f + 1)
                nc.vector.tensor_copy(ssum[:, :], rbank[:, NE:NE + 1]).then_inc(router_read, 1)
                nc.vector.max(top[:, :], logit[:, :]).then_inc(top_step, 1)
                t0 = f * TOP_STEPS
                dve.wait_ge(top_step, t0 + 1)
                nc.vector.tensor_tensor(gap[:, 0:1], top[:, 0:1], top[:, 1:2], ALU.subtract).then_inc(top_step, 1)
                nc.vector.tensor_tensor(gap[:, 1:2], top[:, 1:2], top[:, 0:1], ALU.subtract).then_inc(top_step, 1)
                nc.vector.max_index(top_at[:, :], top[:, :], logit[:, :]).then_inc(top_step, 1)
                wait(dve, top_step, t0 + 4)
                nc.vector.tensor_copy(top_no[:, :], top_at[:, :]).then_inc(top_step, 1)

            def invert_norm(f):
                r0 = f * RN_STEPS
                dve.wait_ge(norm_ready, f + 1)
                nc.vector.tensor_scalar(normf[:, :], norm[:, :], NORM_FLOOR * PART_SCALE, PART_SCALE,
                                        ALU.max, ALU.mult).then_inc(rnorm_step, 1)
                dve.wait_ge(rnorm_step, r0 + 1)
                nc.vector.reciprocal(rnorm[:, :], normf[:, :]).then_inc(rnorm_step, 1)

            def combine(f):
                c0 = f * COMB_STEPS
                dve.wait_ge(wt_ready, f + 1)
                nc.vector.tensor_scalar(wts[:, :], wt[:, :], 1 / PROD_SCALE, None, ALU.mult).then_inc(comb_step, 1)
                dve.wait_ge(top_step, (f + 1) * TOP_STEPS)
                dve.wait_ge(comb_step, c0 + 1)
                for t in range(2):
                    nc.vector.tensor_scalar(pick[:, t, :], expert_no[:, :], top_no[:, t:t + 1], wts[:, t:t + 1],
                                            ALU.is_equal, ALU.mult).then_inc(comb_step, 1)
                wait(dve, comb_step, c0 + 3)
                nc.vector.tensor_tensor(comb[:, :], pick[:, 0, :], pick[:, 1, :], ALU.add).then_inc(comb_step, 1)

            def add_expert(f, e):
                m = f * NE + e
                bank = obank[e % 2]
                dve.wait_ge(o_done, m + 1)
                if e == 0:
                    dve.wait_ge(comb_step, (f + 1) * COMB_STEPS)
                    dve.wait_ge(xres_loaded, 16 * (f + 1))
                if e == NE - 1:
                    wait(dve, out_sent, 16 * f)
                wait(dve, acc_done, m)
                nc.vector.scalar_tensor_tensor(out=(outb if e == NE - 1 else acc)[:, :], in0=bank[:, :],
                                               scalar=comb[:, e:e + 1], in1=(xres if e == 0 else acc)[:, :],
                                               op0=ALU.mult, op1=ALU.add).then_inc(acc_done, 1)

            def block_of(i, parity, gru=True, ffn=True):
                f = i - 1
                for s in range(S):
                    if s == 0 and ffn:
                        split_states(f)
                    if gru:
                        gru_step(i * S + s, s, i, ffn)
                        for c in BIAS_WORK.get(s, ()):
                            bias_gate(i + 1, c)
                        if s == TURN_X_AT:
                            turn_x(i + 2)
                        if s == SPLIT_X_AT:
                            split_x(i + 2)
                    if not ffn:
                        for n in LATE_SPLITS[s]:
                            split_weights(n)
                    if ffn:
                        if s <= 6:
                            split_y(f * NE + s, s)
                        if s == 6:
                            split_y(f * NE + 7, 7)
                        if s == 0:
                            rank_experts(f)
                        if s == 1:
                            invert_norm(f)
                        if s == 2:
                            combine(f)
                        for e in ADD_WORK[s]:
                            add_expert(f, e)

            def prepare_hn_bias():
                dve.wait_ge(hn_bias_loaded, 16 * K)
                nc.vector.tensor_scalar(hn_p[:, 0, :], bias_hn[:, :], PART_SCALE, None, ALU.mult
                                        ).then_inc(hn_bias_step, 1)
                dve.wait_ge(hn_bias_step, 1)
                nc.vector.scalar_tensor_tensor(out=hn_p[:, 1, :], in0=bias_hn[:, :], scalar=PART_SCALE,
                                               in1=hn_p[:, 0, :], op0=ALU.mult, op1=ALU.subtract
                                               ).then_inc(hn_bias_step, 1)

            def prepare_state():
                dve.wait_ge(cond_loaded, 16 * K)
                nc.vector.transpose(cond_t[:, :, :].rearrange("p k c -> p (k c)"), cond_sb[:, :]).then_inc(cond_turned, 1)
                dve.wait_ge(cond_turned, 1)
                nc.vector.tensor_scalar(hist[:, :, S - 1, :], cond_t[:, :, 0:B], PART_SCALE, None, ALU.mult
                                        ).then_inc(h_ready, 1)
                dve.wait_ge(h_ready, 1)
                dve.wait_ge(consts_ready, 3)
                nc.vector.tensor_copy(st[:, 0, 0, :, 0:B], hist[:, :, S - 1, :]).then_inc(hhi_ready, 1)
                dve.wait_ge(hhi_ready, 1)
                nc.vector.tensor_tensor(st[:, 0, 1, :, B:2 * B], hist[:, :, S - 1, :], st[:, 0, 0, :, 0:B],
                                        ALU.subtract).then_inc(both_parts_ready, 1)

            def split_weights(n):
                _, _, src, (hi, lo) = SPLITS[n]
                dve.wait_ge(hi_split, n + 1)
                nc.vector.scalar_tensor_tensor(out=lo, in0=src, scalar=PART_SCALE, in1=hi, op0=ALU.mult,
                                               op1=ALU.subtract).then_inc(weights_split, 1)

            for n in range(N_GRU_SPLITS):
                if n == TURN_X0_AT:
                    turn_x(0)
                if n == SPLIT_X0_AT:
                    split_x(0)
                if n == STATE_AT:
                    prepare_state()
                split_weights(n)
            prepare_hn_bias()
            turn_x(1)
            for c in range(3):
                dve.wait_ge(gi_hi_ready, c + 1)
                nc.vector.scalar_tensor_tensor(out=gi_p[:, 0, 1, :, c, :],
                                               in0=first_gi[c][:, :].rearrange("p (j c) -> p j c", c=P),
                                               scalar=1 / PART_SCALE, in1=gi_p[:, 0, 0, :, c, :],
                                               op0=ALU.mult, op1=ALU.subtract).then_inc(gi_lo_ready, 1)
            split_x(1)
            block_of(0, 0, ffn=False)
            with dve.Fori(0, NB // 2 - 1) as t:
                block_of(t * 2 + 1, 1)
                block_of(t * 2 + 2, 0)
            block_of(NB - 1, 1)
            block_of(NB, 0, gru=False)

        @block.tensor
        def _(pe):
            def inputs_part(b, m0, m1):
                for m in range(m0, m1):
                    c, k, t = m // PER_GATE, m % PER_GATE // len(TERMS), m % len(TERMS)
                    ph, pw = TERMS[t]
                    if m == 0:
                        pe.wait_ge(xhi_ready, b + 1)
                        pe.wait_ge(xlo_ready, b + 1)
                    if m % PER_GATE == 0:
                        wait(pe, gi_biased, 3 * (b - 1) + c)
                    mm = nc.tensor.matmul(gibank[:, :], xp[:, ph, k, :], wih[:, pw, k, GI_GATES[c], :],
                                          start=(m % PER_GATE == 0), stop=((m + 1) % PER_GATE == 0))
                    if (m + 1) % PER_GATE == 0:
                        mm.then_inc(gi_done, 1)

            def start_pair(b, r, block_parity):
                if r == 0:
                    pe.wait_ge(gi_lo_ready, 3 * (b + 1))
                g = gates[r % 2]
                for part in range(2):
                    nc.tensor.matmul(g[:, 3 * P:4 * P], ident[:, :, :, :].rearrange("p j q b -> p (j q b)"),
                                     hn_p[:, part, :], start=(part == 0), stop=False, skip_group_check=True)
                for part in range(2):
                    for j in range(K):
                        mm = nc.tensor.matmul(g[32 * j:32 * j + 32, 0:3 * P],
                                              ident[:, r, :, :].rearrange("p q b -> p (q b)"),
                                              gi_p[:, block_parity, part, j, :, :].rearrange("p g c -> p (g c)"),
                                              start=False, stop=False, skip_group_check=True)
                mm.then_inc(seeds_done, 1)

            def state_part(n, s):
                q, g = s % 2, gates[s // 2 % 2]

                def weights_low(k):
                    for j in range(K):
                        nc.tensor.matmul(g[32 * j:32 * j + 32, P:4 * P], st[:, q, 0, k, :], whh[:, 1, k, j, :],
                                         start=False, stop=False, skip_group_check=True)

                pe.wait_ge(hhi_ready, n + 1)
                weights_low(0)
                pe.wait_ge(both_parts_ready, 2 * (n + 1))
                for k in range(K):
                    for j in range(K):
                        mm = nc.tensor.matmul(high_sum[32 * j:32 * j + 32, 0:G], st[:, q, 1, k, :],
                                              whh[:, 0, k, j, :], start=(k == 0), stop=(k == K - 1),
                                              skip_group_check=True)
                mm.then_inc(products_done, 1)
                for k in range(1, K):
                    weights_low(k)
                pe.wait_ge(low_copied, n + 1)
                nc.tensor.matmul(g[:, P:4 * P], cross[:, q, :, :, :].rearrange("p j q b -> p (j q b)"),
                                 low_sum[:, :], start=False, stop=True, skip_group_check=True
                                 ).then_inc(sums_ready, 1)

            def logits(f):
                pe.wait_ge(hfhi_ready, f + 1)
                pe.wait_ge(hflo_ready, f + 1)
                wait(pe, acc_done, f * NE)
                n = 0
                for k in range(K):
                    for ph, pw in TERMS:
                        mm = nc.tensor.matmul(rbank[:, 0:NE], hf[:, ph, k, :], rw[:, pw, k, :], start=(n == 0),
                                              stop=(n == 3 * K - 1), skip_group_check=True)
                        n += 1
                mm.then_inc(logits_done, 1)

            def sum_squares(f):
                pe.wait_ge(sq_step, (f + 1) * SQ_STEPS)
                nc.tensor.matmul(rbank[:, NE:NE + 1], sqs[:, :], ones[:, :], start=False, stop=True,
                                 skip_group_check=True).then_inc(ssum_done, 1)

            def expert_down(f, e):
                m = f * NE + e
                wait(pe, ylo_ready, m - 1 if e else m)
                n = 0
                for k in range(K):
                    for ph, pw in TERMS:
                        mm = nc.tensor.matmul(ybank[e % 2][:, 0:P], wa[:, pw, k, e, :], hf[:, ph, k, :],
                                              start=(n == 0), stop=(n == 3 * K - 1))
                        n += 1
                mm.then_inc(y_done, 1)

            def expert_up(f, e):
                m = f * NE + e
                bank = obank[e % 2]
                pe.wait_ge(ylo_ready, m + 1)
                wait(pe, acc_done, m - 1 if e else m)
                for n, (ph, pw) in enumerate(TERMS):
                    mm = nc.tensor.matmul(bank[:, :], y[:, e % 2, ph, :], wb[:, pw, e, :], start=(n == 0),
                                          stop=(n == 2))
                mm.then_inc(o_done, 1)

            def block_of(i, parity, gru=True, ffn=True):
                f = i - 1
                for s in range(S):
                    n = i * S + s
                    if gru:
                        state_part(n, s)
                        if s in SEED_WORK:
                            r = SEED_WORK[s] % (S // 2)
                            start_pair(i if r else i + 1, r, parity if r else 1 - parity)
                    if ffn and s == 0:
                        logits(f)
                    if ffn and s <= 6:
                        expert_down(f, s)
                    if gru:
                        ahead, m0, m1 = GI_WORK[s]
                        inputs_part(i + ahead, 0 if s == 0 and not ffn else m0, m1)
                    if ffn and s == (0 if gru else 1):
                        sum_squares(f)
                    if ffn and s >= 1:
                        expert_up(f, s - 1)
                    if ffn and s == 6:
                        expert_down(f, 7)
                    if ffn and s == 7:
                        expert_up(f, 7)

            def spread_bias(c):
                mm = nc.tensor.matmul(first_gi[c][:, :], scale_rows[:, :], bias_rows[:, GI_GATES[c], :], start=True,
                                      stop=True, skip_group_check=True)
                mm.then_inc(bias_spread, 1)

            def first_inputs():
                for at, k in enumerate(IH_ORDER):
                    pe.wait_ge(weights_split, IH_SPLIT[at])
                    for c in range(3):
                        if at == 0:
                            pe.wait_ge(bias_copied, c + 1)
                        for ph, pw in TERMS:
                            mm = nc.tensor.matmul(first_gi[c][:, :], xp[:, ph, k, :], wih[:, pw, k, GI_GATES[c], :],
                                                  start=False, stop=False, skip_group_check=True)
                        if at == K - 1:
                            mm.then_inc(gi_done, 1)

            pe.wait_ge(consts_ready, N_MEMSETS)
            pe.wait_ge(bias_loaded, 16 * 2)
            for c in range(3):
                spread_bias(c)
            pe.wait_ge(xhi_ready, 1)
            pe.wait_ge(xlo_ready, 1)
            first_inputs()
            pe.wait_ge(consts_ready, N_CONST)
            pe.wait_ge(hn_bias_step, 2)
            pe.wait_ge(weights_split, N_GRU_SPLITS)
            start_pair(0, 0, 0)
            block_of(0, 0, ffn=False)
            pe.wait_ge(weights_split, len(SPLITS))
            with pe.Fori(0, NB // 2 - 1) as t:
                block_of(t * 2 + 1, 1)
                block_of(t * 2 + 2, 0)
            block_of(NB - 1, 1)
            block_of(NB, 0, gru=False)


_INS = ['x', 'cond_2048', 'L0_cond_W_ih', 'L0_cond_W_hh', 'L0_cond_b_ih', 'L0_cond_b_hh', 'L0_ffn_router_w',
        'L0_ffn_Wa', 'L0_ffn_Wb']


def kernel(**inputs):
    import numpy as np
    import concourse.bacc as bacc
    from concourse.bass_utils import run_bass_kernel_spmd

    nc = bacc.Bacc("TRN2", target_bir_lowering=False, num_devices=1)
    arrays, args = {}, []
    for name in _INS:
        a = np.ascontiguousarray(inputs[name])
        arrays[f"in_{name}"] = a
        args.append(nc.dram_tensor(f"in_{name}", a.shape, mybir.dt.from_np(a.dtype), kind="ExternalInput").ap())
    shape = inputs['x'].shape
    args.append(nc.dram_tensor("out_0", shape, F32, kind="ExternalOutput").ap())
    gru_moe_kernel(nc, *args)
    return run_bass_kernel_spmd(nc, [arrays], core_ids=[0]).results[0]["out_0"]
```
